# Optimizing a Trainium2 kernel written in Bass

```python
import numpy as np
import jax
import jax.numpy as jnp

def _softmax(x, axis=-1):
    return jax.nn.softmax(x, axis=axis)

def _gelu(x):
    return jax.nn.gelu(x, approximate=True)

def _silu(x):
    return jax.nn.silu(x)

def _sigmoid(x):
    return jax.nn.sigmoid(x)

def _layernorm(x, axis=-1, eps=1e-05):
    m = jnp.mean(x, axis=axis, keepdims=True)
    v = jnp.var(x, axis=axis, keepdims=True)
    return (x - m) / jnp.sqrt(v + eps)

def _scatter_add(tgt, idx, src, axis=0):
    return tgt.at[idx].add(src)

def _segment_sum(src, seg, n):
    return jax.ops.segment_sum(src, seg, n)
kernel_name = 'mk_hybrid_d1_jaxref_r8_5056f5'

def setup_inputs(seed: int=0):
    np.random.seed(seed)
    _w = jnp.asarray

    def _L0_attn_a_setup():
        import jax, jax.numpy as jnp
        import numpy as np
        B, T = (4, 256)
        D_MODEL = 128
        N_HEADS = 8
        HEAD_DIM = 32
        KV_LRANK = 64

        def _orthogonalize_per_head(w):
            chunks = w.reshape(N_HEADS, HEAD_DIM, D_MODEL)

            def ns(m):
                A = m @ m.T
                Bm = 1.5 * jnp.eye(HEAD_DIM, dtype=m.dtype) - 0.5 * A
                return Bm @ m
            return jax.vmap(ns)(chunks).reshape(w.shape)
        key = jax.random.key(seed)
        ks = jax.random.split(key, 6)

        def lin(k, out_dim, in_dim):
            bound = 1.0 / np.sqrt(in_dim)
            return jax.random.uniform(k, (out_dim, in_dim), jnp.float32, -bound, bound)
        Wq = _orthogonalize_per_head(lin(ks[0], N_HEADS * HEAD_DIM, D_MODEL))
        return {'x': jax.random.normal(ks[1], (B, T, D_MODEL), jnp.float32), 'Wq': Wq, 'Wkv_down': lin(ks[2], KV_LRANK, D_MODEL), 'Wk_up': lin(ks[3], N_HEADS * HEAD_DIM, KV_LRANK), 'Wv_up': lin(ks[4], N_HEADS * HEAD_DIM, KV_LRANK), 'Wo': lin(ks[5], D_MODEL, N_HEADS * HEAD_DIM)}
    _L0_attn_a_in = _L0_attn_a_setup()

    def _L0_attn_b_setup():
        import jax, jax.numpy as jnp
        import numpy as np
        NUM_HEADS = 16
        key = jax.random.key(seed)
        ks = jax.random.split(key, 5)
        B, S, H = (2, 256, 128)
        scale = 0.02
        return {'x': jax.random.normal(ks[0], (B, S, H), dtype=jnp.float32), 'w_qkv': jax.random.normal(ks[1], (H, 3 * H), dtype=jnp.float32) * scale, 'b_qkv': jax.random.normal(ks[2], (3 * H,), dtype=jnp.float32) * scale, 'w_out': jax.random.normal(ks[3], (H, H), dtype=jnp.float32) * scale, 'b_out': jax.random.normal(ks[4], (H,), dtype=jnp.float32) * scale}
    _L0_attn_b_in = _L0_attn_b_setup()

    def _L0_ffn_setup():
        import jax, jax.numpy as jnp
        import numpy as np
        TOP_K = 2

        def _swiglu_mlp(x, wgu, wd, inter):
            gu = x @ wgu
            a = jax.nn.silu(gu[:, :inter]) * gu[:, inter:]
            return a @ wd
        key = jax.random.key(seed)
        ks = jax.random.split(key, 6)
        H, I, E = (128, 352, 8)
        B, S = (2, 128)
        w = 0.02
        return {'x': jax.random.normal(ks[0], (B, S, H), jnp.float32), 'gate_w': jax.random.normal(ks[1], (H, E), jnp.float32) * w, 'base_wgu': jax.random.normal(ks[2], (H, 2 * I), jnp.float32) * w, 'base_wd': jax.random.normal(ks[3], (I, H), jnp.float32) * w, 'exp_wgu': jax.random.normal(ks[4], (E, H, 2 * I), jnp.float32) * w, 'exp_wd': jax.random.normal(ks[5], (E, I, H), jnp.float32) * w}
    _L0_ffn_in = _L0_ffn_setup()
    _d = {'L0_attn_a_x': _L0_attn_a_in['x'], 'L0_attn_a_Wq': _L0_attn_a_in['Wq'], 'L0_attn_a_Wkv_down': _L0_attn_a_in['Wkv_down'], 'L0_attn_a_Wk_up': _L0_attn_a_in['Wk_up'], 'L0_attn_a_Wv_up': _L0_attn_a_in['Wv_up'], 'L0_attn_a_Wo': _L0_attn_a_in['Wo'], 'L0_attn_b_w_qkv': _L0_attn_b_in['w_qkv'], 'L0_attn_b_b_qkv': _L0_attn_b_in['b_qkv'], 'L0_attn_b_w_out': _L0_attn_b_in['w_out'], 'L0_attn_b_b_out': _L0_attn_b_in['b_out'], 'L0_ffn_gate_w': _L0_ffn_in['gate_w'], 'L0_ffn_base_wgu': _L0_ffn_in['base_wgu'], 'L0_ffn_base_wd': _L0_ffn_in['base_wd'], 'L0_ffn_exp_wgu': _L0_ffn_in['exp_wgu'], 'L0_ffn_exp_wd': _L0_ffn_in['exp_wd']}
    _x0 = _d['L0_attn_a_x']
    _d['L0_attn_a_x'] = jax.random.normal(jax.random.fold_in(jax.random.key(seed), 1), (1, 2048, 128), dtype=_x0.dtype)
    del _x0
    return _d

def reference(L0_attn_a_x, L0_attn_a_Wq, L0_attn_a_Wkv_down, L0_attn_a_Wk_up, L0_attn_a_Wv_up, L0_attn_a_Wo, L0_attn_b_w_qkv, L0_attn_b_b_qkv, L0_attn_b_w_out, L0_attn_b_b_out, L0_ffn_gate_w, L0_ffn_base_wgu, L0_ffn_base_wd, L0_ffn_exp_wgu, L0_ffn_exp_wd):

    def _L0_attn_a_ref(x, Wq, Wkv_down, Wk_up, Wv_up, Wo):
        import jax, jax.numpy as jnp
        import numpy as np
        B, T = (4, 256)
        D_MODEL = 128
        N_HEADS = 8
        HEAD_DIM = 32
        KV_LRANK = 64

        def _orthogonalize_per_head(w):
            chunks = w.reshape(N_HEADS, HEAD_DIM, D_MODEL)

            def ns(m):
                A = m @ m.T
                Bm = 1.5 * jnp.eye(HEAD_DIM, dtype=m.dtype) - 0.5 * A
                return Bm @ m
            return jax.vmap(ns)(chunks).reshape(w.shape)
        b, t, _ = x.shape
        q = (x @ Wq.T).reshape(b, t, N_HEADS, HEAD_DIM)
        kv_latent = x @ Wkv_down.T
        k = (kv_latent @ Wk_up.T).reshape(b, t, N_HEADS, HEAD_DIM)
        v = (kv_latent @ Wv_up.T).reshape(b, t, N_HEADS, HEAD_DIM)
        scale = HEAD_DIM ** (-0.5)
        scores = jnp.einsum('bqhd,bkhd->bhqk', q, k) * scale
        attn = jax.nn.softmax(scores, axis=-1)
        out = jnp.einsum('bhqk,bkhd->bqhd', attn, v)
        out = out.reshape(b, t, N_HEADS * HEAD_DIM)
        return out @ Wo.T

    def _L0_attn_b_ref(x, w_qkv, b_qkv, w_out, b_out):
        import jax, jax.numpy as jnp
        import numpy as np
        NUM_HEADS = 16
        B, S, H = x.shape
        nh = NUM_HEADS
        hd = H // nh
        attn_scale = 1.0 / np.sqrt(hd).astype(np.float32)
        qkv = x @ w_qkv + b_qkv
        q, k, v = jnp.split(qkv, 3, axis=-1)
        to_heads = lambda t: t.reshape(B, S, nh, hd).transpose(0, 2, 1, 3)
        q, k, v = (to_heads(q), to_heads(k), to_heads(v))
        scores = jnp.einsum('bhid,bhjd->bhij', q, k) * attn_scale
        i = jnp.arange(S)[:, None]
        j = jnp.arange(S)[None, :]
        scores = jnp.where(j >= i, scores, -jnp.inf)
        attn = jax.nn.softmax(scores, axis=-1)
        out = jnp.einsum('bhij,bhjd->bhid', attn, v)
        out = out.transpose(0, 2, 1, 3).reshape(B, S, H)
        return out @ w_out + b_out

    def _L0_ffn_ref(x, gate_w, base_wgu, base_wd, exp_wgu, exp_wd):
        import jax, jax.numpy as jnp
        import numpy as np
        TOP_K = 2

        def _swiglu_mlp(x, wgu, wd, inter):
            gu = x @ wgu
            a = jax.nn.silu(gu[:, :inter]) * gu[:, inter:]
            return a @ wd
        orig_shape = x.shape
        H = orig_shape[-1]
        I = base_wd.shape[0]
        E = gate_w.shape[1]
        xt = x.reshape(-1, H)
        T = xt.shape[0]
        base_y = _swiglu_mlp(xt, base_wgu, base_wd, I)
        logits = xt @ gate_w
        probs = jax.nn.softmax(logits.astype(jnp.float32), axis=-1)
        topw, topi = jax.lax.top_k(probs, TOP_K)
        topw = topw / jnp.sum(topw, axis=-1, keepdims=True)
        topw = topw.astype(x.dtype)
        cw = jnp.zeros((T, E), x.dtype).at[jnp.arange(T)[:, None], topi].add(topw)
        out = base_y
        for e in range(E):
            ye = _swiglu_mlp(xt, exp_wgu[e], exp_wd[e], I)
            out = out + cw[:, e:e + 1] * ye
        return out.reshape(orig_shape)
    x = L0_attn_a_x
    x = x + _L0_attn_a_ref(_layernorm(x, axis=-1), L0_attn_a_Wq, L0_attn_a_Wkv_down, L0_attn_a_Wk_up, L0_attn_a_Wv_up, L0_attn_a_Wo)
    x = x + _L0_ffn_ref(_layernorm(x, axis=-1), L0_ffn_gate_w, L0_ffn_base_wgu, L0_ffn_base_wd, L0_ffn_exp_wgu, L0_ffn_exp_wd)
    x = x + _L0_attn_b_ref(_layernorm(x, axis=-1), L0_attn_b_w_qkv, L0_attn_b_b_qkv, L0_attn_b_w_out, L0_attn_b_b_out)
    x = x + _L0_ffn_ref(_layernorm(x, axis=-1), L0_ffn_gate_w, L0_ffn_base_wgu, L0_ffn_base_wd, L0_ffn_exp_wgu, L0_ffn_exp_wd)
    return x

_drawn_inputs = setup_inputs


def setup_inputs(seed=0):
    import zlib

    import numpy as np

    out = dict(_drawn_inputs(seed))
    spreads = {}
    factors = {'L0_attn_a_Wq': 7.314,
     'L0_attn_a_Wkv_down': 8.0,
     'L0_attn_a_Wk_up': 7.314,
     'L0_attn_a_Wv_up': 6.286,
     'L0_attn_a_Wo': 6.334,
     'L0_attn_b_w_qkv': 29.084,
     'L0_attn_b_b_qkv': 64.0,
     'L0_attn_b_w_out': 8.0,
     'L0_attn_b_b_out': 177.216,
     'L0_ffn_gate_w': 16.628,
     'L0_ffn_base_wgu': 20.656,
     'L0_ffn_base_wd': 20.927,
     'L0_ffn_exp_wgu': 13.084,
     'L0_ffn_exp_wd': 13.014}
    for name, (base, spread) in spreads.items():
        noise = np.random.default_rng([zlib.crc32(name.encode()), seed]).standard_normal(out[name].shape)
        drawn = base * np.exp(spread * noise) if base else spread * noise
        out[name] = jnp.asarray(drawn.astype(out[name].dtype))
    for name, factor in factors.items():
        out[name] = (out[name] * factor).astype(out[name].dtype)
    return out
```

```python
import numpy as np
import concourse.bass as bass
from concourse import mybir
from contextlib import ExitStack

F32 = mybir.dt.float32
F32R = mybir.dt.float32r
U32 = mybir.dt.uint32
ALU = mybir.AluOpType
ACT = mybir.ActivationFunctionType
AX = mybir.AxisListType

P = 128
T, D = 2048, 128
NT = T // P
QC = 512
NC = T // QC
TPC = QC // P
G = 4
HA, DA, RANK = 8, 32, 64
HB, DB = 16, 8
GA, GB = HA // G, HB // G
E, I = 8, 352
FT = [(0, 128), (128, 128), (256, 96)]
EPS = 1e-5
MASKED = -1e38
SA = 32
CA = 3 * SA
KA_ROWS = CA + 2
CB = 3 * DB
LN_EXP = 2

C_ID, C_SEL, C_MT, C_MQ, C_COL = 0, 128, 256, 384, 512
COLS = ["lo_qa", "lo_ka", "lo_lat", "neg_ka", "lo_qb", "lo_kb", "neg_kb", "zero"]
C_IOTA = C_COL + len(COLS)
C_ALL = C_IOTA + E


def constants():
    c = np.zeros((P, C_ALL), np.float32)
    r = np.arange(P)
    c[:, C_ID:C_ID + P] = np.eye(P)
    c[32 * (r // 32) + DB, C_SEL + r] = 1.0
    c[:, C_MT:C_MT + P] = np.where(r[None, :] > r[:, None], MASKED, 0)
    c[:, C_MQ:C_MQ + P] = np.where(r[None, :] < r[:, None], MASKED, 0)
    cols = {
        "lo_qa": (r // SA == 1),
        "lo_ka": (r // SA == 2),
        "lo_lat": (r >= RANK),
        "neg_ka": -1.0 * ((r == CA) | (r == CA + 1)),
        "lo_qb": (r % 32 // DB == 1),
        "lo_kb": (r % 32 // DB == 2),
        "neg_kb": -1.0 * ((r % 32 == CB) | (r % 32 == CB + 1)),
        "zero": 0 * r,
    }
    for i, n in enumerate(COLS):
        c[:, C_COL + i] = cols[n]
    c[:, C_IOTA:C_IOTA + E] = np.arange(E)[None, :]
    return c


class Order:

    def __init__(self, kind):
        self.kind = kind
        self.a = kind == "A"
        self.groups = GA if self.a else GB
        if self.a:
            self.steps = [(g, c) for g in range(GA) for c in range(NC)]
        else:
            self.steps = [(g, c) for g in range(GB) for c in (range(NC) if g % 2 else reversed(range(NC)))]
        self.events, self.at, self.uses = [], {}, 0
        self.tiles, self.tile_at, self.pairs, self.pair_at, self.projections = 0, {}, 0, {}, 0
        self.proj_at, self.last_tile_of_group, self.last_pair_of_group = {}, {}, {}
        self.build()

    def key_tiles(self, n):
        g, c = self.steps[n]
        if self.a:
            ks = [(k, QC, False) for k in range(NT)]
        else:
            ks = [(c * TPC + d, (d + 1) * P, True) for d in reversed(range(TPC))]
            ks += [(k, QC, False) for k in range((c + 1) * TPC, NT)]
        return [ks[i:i + 2] for i in range(0, len(ks), 2)]

    def first_key_chunk(self, n):
        return 0 if self.a else self.steps[n][1]

    def ring(self, *use):
        self.at[use] = self.uses
        self.uses += 1
        if use[0] in ("q", "k", "lat"):
            self.proj_at[use] = self.projections
            self.projections += 1
        self.events.append(("ring", use))

    def for_group(self, g):
        if self.a:
            return [("k", g, h, c) for c in range(NC) for h in range(G)] + [("v", g, c) for c in range(NC)]
        return [("k", g, 0, c) for c in range(NC)] + [("v", g, c) for c in range(NC)]

    def for_queries(self, n):
        heads = range(G)
        kcs = range(self.first_key_chunk(n), NC)
        out = [("q", n, h) for h in (heads if self.a else [0])]
        for h in heads:
            out += [("max", n, h, q, k) for q in range(TPC) for k in kcs]
            if self.a and h:
                out.insert(len(out) - len(kcs) * TPC + 3, ("shift", n, h - 1))
        if self.a:
            out.append(("shift", n, G - 1))
        else:
            out.append(("shift", n, 0))
        return out

    def build(self):
        if self.a:
            for c in range(NC):
                self.ring("lat", c)
        for use in self.for_group(0) + self.for_queries(0):
            self.ring(*use)
        last = len(self.steps) - 1
        for n, (g, c) in enumerate(self.steps):
            pairs = self.key_tiles(n)
            units = G * len(pairs)
            first_of_group = [s[0] for s in self.steps].index(g)
            todo = []
            if g + 1 < self.groups:
                new = self.for_group(g + 1)
                i = n - first_of_group
                if self.a:
                    share = -(-len(new) // (NC - 1))
                    todo += new[i * share:(i + 1) * share]
                elif i == 1:
                    todo += new
            if n < last:
                todo += self.for_queries(n + 1)
            done, extra = 0, []
            for u in range(units):
                k, h = divmod(u, G)
                self.events.append(("scores", n, k, h))
                self.tile_at[n, k, h] = self.tiles
                self.tiles += 1
                for use in extra:
                    self.ring(*use)
                extra = []
                want = min(len(todo), -(-len(todo) * (u + 1) // max(1, int(units * 0.88))))
                while done < want:
                    self.ring(*todo[done])
                    done += 1
                if h == G - 1:
                    if k == 0 and n:
                        self.product(n - 1, len(self.key_tiles(n - 1)) - 1)
                        self.events.append(("evacuate", n - 1))
                        extra = [] if self.a else [("sums", n - 1)]
                    if k >= 1:
                        self.product(n, k - 1)
                if n and u == G + 1:
                    extra = [("out", n - 1)]
            for use in extra + todo[done:]:
                self.ring(*use)
            self.last_tile_of_group[g] = self.tiles
            self.last_pair_of_group[g] = self.pairs + 1
        self.product(last, len(self.key_tiles(last)) - 1)
        self.events.append(("evacuate", last))
        if not self.a:
            self.ring("sums", last)
        self.ring("out", last)

    def product(self, n, k):
        self.pair_at[n, k] = self.pairs
        self.pairs += 1
        self.events.append(("product", n, k))


def build(nc, x_in, wq_a, wkv_a, wk_a, wv_a, wo_a, wq_b, wk_b, wv_b, bq_b, bk_b, bv_b, wo_b, bo_b,
          gate_w, base_wgu, base_wd, exp_wgu, exp_wd, consts, out):
    orders = {"A": Order("A"), "B": Order("B")}
    ctx = ExitStack()
    with ctx:
        def sb(name, shape, dt=F32):
            return ctx.enter_context(nc.sbuf_tensor(name, shape, dt))

        def sem(name):
            return ctx.enter_context(nc.semaphore(name))

        cst = sb("cst", [P, C_ALL])
        ident = cst[:, C_ID:C_ID + P]
        sel = cst[:, C_SEL:C_SEL + P]
        identr = sb("identr", [P, P], F32R)
        maskr = sb("maskr", [P, 2, P], F32R)
        ones = sb("ones", [P, 32])
        x = sb("x", [P, NT, D])
        xh = sb("xh", [P, T], F32R)
        xl = sb("xl", [P, T], F32R)
        kst = sb("kst", [P, 2, G, T], F32R)
        qst = sb("qst", [P, 2, G, QC], F32R)
        vst = sb("vst", [P, 2, NT, P])
        prob = sb("prob", [P, 8, 2 * QC])
        tmp = sb("tmp", [P, 2, QC], F32R)
        flat = sb("flat", [P, T], F32R)
        mx = sb("mx", [P, 2, TPC, NC])
        mq = sb("mq", [P, 2, G, TPC])
        ct = sb("ct", [P, 2, TPC, P], F32R)
        o_sb = sb("o_sb", [P, QC])
        rinv = sb("rinv", [P, QC])
        ot = sb("ot", [P, 2, QC])
        spare = prob[:].rearrange("p a n -> p (a n)")

        def in_spare(at, *shape):
            n = int(np.prod(shape))
            names = "abc"[:len(shape)]
            a = spare[:, at:at + n]
            if len(shape) == 1:
                return a
            return a.rearrange(f"p ({' '.join(names)}) -> p {' '.join(names)}", **dict(zip(names, shape)))

        xn = in_spare(8 * QC, NT, D)

        stats = sb("stats", [P, NT, 6])
        mv = sb("mv", [P, NT, 2])
        marker = sb("marker", [P, 2])
        sd = sb("sd", [P, NT])
        rs = sb("rs", [P, NT])
        sc1 = sb("sc1", [P, NT])
        wq_raw, wqh, wql = in_spare(0, HA, KA_ROWS), sb("wqh", [P, HA, KA_ROWS], F32R), sb("wql", [P, HA, KA_ROWS], F32R)
        wk_raw, wkh, wkl = in_spare(1024, HA, KA_ROWS), sb("wkh", [P, HA, KA_ROWS], F32R), sb("wkl", [P, HA, KA_ROWS], F32R)
        wv_raw, wvh, wvl = sb("wv_raw", [P, HA * DA]), sb("wvh", [P, HA * DA], F32R), sb("wvl", [P, HA * DA], F32R)
        wc_raw, wch, wcl = sb("wc_raw", [P, P]), sb("wch", [P, P], F32R), sb("wcl", [P, P], F32R)
        wo_a_sb = sb("wo_a_sb", [P, GA, D])
        wqb_raw, wkb_raw, wvb_raw = (a.rearrange("p (g n) -> p g n", n=P) for a in (o_sb[:], rinv[:], ot[:, 0, :]))
        wvb_raw = wvb_raw[:, 0, :]
        wqbh, wqbl, wkbh, wkbl = (w[:].rearrange("p h n -> p (h n)")[:, 0:GB * P].rearrange("p (g n) -> p g n", n=P)
                                  for w in (wqh, wql, wkh, wkl))
        wvbh, wvbl = wch[:], wcl[:]
        wo_b_sb = sb("wo_b_sb", [P, GB, D])
        bias = sb("bias", [P, 4, GB])
        bv_sb = sb("bv_sb", [P, D])
        bo_sb = sb("bo_sb", [P, D])
        gw_raw, gwh, gwl = sb("gw_raw", [P, E]), sb("gwh", [P, E], F32R), sb("gwl", [P, E], F32R)
        wgu = in_spare(13 * QC, 2, 2 * I)
        queries_flat = qst[:].rearrange("p a h n -> p (a h n)")
        wguh, wgul = (queries_flat[:, i * 4 * I:(i + 1) * 4 * I].rearrange("p (a n) -> p a n", a=2) for i in range(2))
        wd = sb("wd", [P, 2, len(FT), D])
        silu = in_spare(0, 2, QC)
        hid = in_spare(2 * QC, 2, len(FT), QC)
        lg, pr, top, cw2 = (in_spare(12 * QC + i * P, NT, E) for i in range(4))
        lmax = sb("lmax", [P, NT])
        topi = sb("topi", [P, NT, 8], U32)
        topf = sb("topf", [P, NT, 2])
        wtop = sb("wtop", [P, NT, 2])
        cw = sb("cw", [P, NT, E])

        ps = ctx.enter_context(nc.psum_tensor("ps", [P, 8, QC], F32))
        ring_banks = {"A": [4, 5], "B": [4, 5, 7]}

        def bank_of(kind, m):
            return ring_banks[kind][m % len(ring_banks[kind])]

        def col(name, rows=P):
            i = C_COL + COLS.index(name)
            return cst[0:rows, i:i + 1]

        loaded = {n: sem("loaded_" + n) for n in ("cst", "x", "qa", "ca", "ka", "va", "small", "b")}
        weights_split = sem("weights_split")
        filled = sem("filled")
        S = {}
        for kind in "AB":
            for n in ("scores_ready", "exp_done", "product_done", "ring_full", "ring_free",
                      "high_ready", "evacuated", "shift_parts", "keys_ready"):
                S[kind, n] = sem(n + "_" + kind)
        chain = sem("vector_chain")
        var_ready, root_ready = sem("var_ready"), sem("root_ready")
        norm_ready, turned, high_done, parts_done = sem("norm_ready"), sem("turned"), sem("high_done"), sem("parts_done")
        logits_ready, logits_shifted, exp_logits, routed = sem("logits_ready"), sem("logits_shifted"), sem("exp_logits"), sem("routed")
        gu_loaded = [sem("gu_loaded0"), sem("gu_loaded1")]
        gu_split, gate_ready, up_ready, silu_done, hidden_ready, down_ready, added = (
            sem(n) for n in ("gu_split", "gate_ready", "up_ready", "silu_done", "hidden_ready", "down_ready", "added"))
        stored = sem("stored")
        attention_done, biases_ready = sem("attention_done"), sem("biases_ready")

        NEXP = E + 1
        UNITS = NEXP * NC
        SPLITS = ["wc", "wq", "wk", "wv", "gw", "wqb", "wkb", "wvb"]

        def split_count(name):
            return 2 * (SPLITS.index(name) + 1)

        block = ctx.enter_context(nc.Block())

        @block.sync
        def _(sp):
            sp.dma_start(cst[:], consts).then_inc(loaded["cst"], 16)
            for c in range(NC):
                sp.dma_start(x[:, c * TPC:(c + 1) * TPC, :],
                             x_in[c * QC:(c + 1) * QC, :].rearrange("(t p) d -> p t d", p=P)).then_inc(loaded["x"], 16)
            sp.dma_start(wc_raw[:], wkv_a).then_inc(loaded["ca"], 16)
            sp.dma_start(wq_raw, wq_a).then_inc(loaded["qa"], 16)
            sp.dma_start(wk_raw, wk_a).then_inc(loaded["ka"], 16)
            sp.dma_start(wv_raw[:], wv_a).then_inc(loaded["va"], 16)
            sp.dma_start(wo_a_sb[:], wo_a).then_inc(loaded["small"], 16)
            sp.dma_start(gw_raw[:], gate_w).then_inc(loaded["small"], 16)
            sp.wait_ge(attention_done, 1)
            for dst, src in ((wqb_raw, wq_b), (wkb_raw, wk_b), (wvb_raw[:], wv_b), (wo_b_sb[:], wo_b),
                             (bias[:, 0, :], bq_b), (bias[:, 1, :], bk_b)):
                sp.dma_start(dst, src).then_inc(loaded["b"], 16)
            sp.dma_start(bv_sb[:], bv_b.broadcast_to([P, D])).then_inc(loaded["b"], 16)
            sp.dma_start(bo_sb[:], bo_b.broadcast_to([P, D])).then_inc(loaded["b"], 16)

            def load_expert(n, gu, down):
                par = n % 2
                if n >= 2:
                    sp.wait_ge(gu_split, 2 * (n - 1))
                    sp.wait_ge(down_ready, NC * (n - 1))
                sp.dma_start(wgu[:, par, :], gu).then_inc(gu_loaded[par], 16)
                sp.dma_start(wd[:, par, 0:2, :], down[0:256, :].rearrange("(f p) d -> p f d", p=P)).then_inc(gu_loaded[par], 16)
                sp.dma_start(wd[0:96, par, 2, :], down[256:I, :]).then_inc(gu_loaded[par], 16)

            def load_experts(r):
                load_expert(NEXP * r, base_wgu, base_wd)
                for e in range(E):
                    load_expert(NEXP * r + e + 1, exp_wgu[e], exp_wd[e])

            load_experts(0)
            od = orders["B"]
            for g in range(GB):
                sp.wait_ge(S["B", "ring_free"], od.at["k", g, 0, NC - 1] + 1)
                if g == 0:
                    sp.wait_ge(filled, 5)
                if g >= 2:
                    sp.wait_ge(S["B", "scores_ready"], od.last_tile_of_group[g - 2])
                for h in range(G):
                    sp.dma_start(kst[32 * h:32 * h + 32, g % 2, h, :].bitcast(F32),
                                 flat[32 * h:32 * h + 32, :].bitcast(F32)).then_inc(S["B", "keys_ready"], 16)
            sp.wait_ge(attention_done, 2)
            load_experts(1)
            for c in range(NC):
                sp.wait_ge(added, NEXP * NC + (NEXP - 1) * NC + c + 1)
                sp.dma_start(out[c * QC:(c + 1) * QC, :].rearrange("(t p) d -> p t d", p=P),
                             x[:, c * TPC:(c + 1) * TPC, :]).then_inc(stored, 16)
            sp.wait_ge(stored, 16 * NC)

        @block.gpsimd
        def _(pool):
            n_split = [0]

            def split(hi, lo, raw):
                nc.gpsimd.tensor_copy(hi, raw).then_inc(weights_split, 1)
                n_split[0] += 1
                pool.wait_ge(weights_split, n_split[0])
                nc.gpsimd.tensor_tensor(lo, raw, hi.bitcast(F32), ALU.subtract).then_inc(weights_split, 1)
                n_split[0] += 1

            nc.gpsimd.memset(ones[:], 1.0).then_inc(filled, 1)
            nc.gpsimd.memset(ct[:].bitcast(F32), 0.0).then_inc(filled, 1)
            pool.wait_ge(loaded["ca"], 16)
            split(wch[:], wcl[:], wc_raw[:])
            pool.wait_ge(loaded["qa"], 16)
            split(wqh[:], wql[:], wq_raw)
            pool.wait_ge(loaded["ka"], 16)
            split(wkh[:], wkl[:], wk_raw)
            pool.wait_ge(loaded["va"], 16)
            split(wvh[:], wvl[:], wv_raw[:])
            pool.wait_ge(loaded["small"], 32)
            split(gwh[:], gwl[:], gw_raw[:])

            def split_expert(n):
                par = n % 2
                pool.wait_ge(gu_loaded[par], 48 * (n // 2 + 1))
                if n >= 2:
                    pool.wait_ge(up_ready, len(FT) * NC * (n - 1))
                nc.gpsimd.tensor_copy(wguh[:, par, :], wgu[:, par, :]).then_inc(gu_split, 1)
                pool.wait_ge(gu_split, 2 * n + 1)
                nc.gpsimd.tensor_tensor(wgul[:, par, :], wgu[:, par, :], wguh[:, par, :].bitcast(F32),
                                        ALU.subtract).then_inc(gu_split, 1)

            pool.wait_ge(attention_done, 1)
            for n in range(2):
                split_expert(n)
            nc.gpsimd.memset(ct[:].bitcast(F32), 0.0).then_inc(filled, 1)
            nc.gpsimd.memset(vst[:], 1.0).then_inc(filled, 1)
            nc.gpsimd.memset(kst[:].bitcast(F32), 0.0).then_inc(filled, 1)
            pool.wait_ge(loaded["b"], 128)
            split(wqbh[:], wqbl[:], wqb_raw)
            split(wkbh[:], wkbl[:], wkb_raw)
            split(wvbh[:], wvbl[:], wvb_raw[:])
            for n in range(2, NEXP):
                split_expert(n)
            for n in range(NEXP, 2 * NEXP):
                split_expert(n)

        @block.scalar
        def _(act):
            def norm(r):
                act.wait_ge(var_ready, r + 1)
                nc.scalar.activation(sd[:], sc1[:], ACT.Sqrt).then_inc(root_ready, 1)
                for c in range(NC):
                    act.wait_ge(turned, NC * r + c + 1)
                    nc.scalar.activation(xh[:, c * QC:(c + 1) * QC], ps[:, c, :], ACT.Identity).then_inc(high_done, 1)

            def attention(kind):
                od = orders[kind]
                bias_cols = {"q": lambda g: bias[:, 2, g:g + 1], "k": lambda g: bias[:, 3, g:g + 1]}
                for ev in od.events:
                    if ev[0] == "scores":
                        _, n, k, h = ev
                        t = od.tile_at[n, k, h]
                        width = sum(w for _, w, _ in od.key_tiles(n)[k])
                        act.wait_ge(S[kind, "scores_ready"], t + 1)
                        if t >= 8:
                            act.wait_ge(S[kind, "product_done"], t // G - 1)
                        b = 2 * (t % 2)
                        nc.scalar.activation(prob[:, t % 8, 0:width],
                                             ps[:, b:b + 2, :].rearrange("p b n -> p (b n)")[:, 0:width], ACT.Exp,
                                             scale=float((DA if od.a else DB) ** -0.5)).then_inc(S[kind, "exp_done"], 1)
                    elif ev[0] == "ring" and ev[1] in od.proj_at:
                        use = ev[1]
                        m, j = od.at[use], od.proj_at[use]
                        rows = P if (use[0] == "lat" or not od.a) else KA_ROWS
                        act.wait_ge(S[kind, "ring_full"], m + 1)
                        if j >= 2:
                            before = [u for u, i in od.proj_at.items() if i == j - 2][0]
                            act.wait_ge(S[kind, "ring_free"], od.at[before] + 1)
                        if od.a:
                            mark = col({"q": "lo_qa", "k": "lo_ka", "lat": "lo_lat"}[use[0]], rows)
                            add = 0.0
                        else:
                            g = od.steps[use[1]][0] if use[0] == "q" else use[1]
                            mark = col("lo_qb" if use[0] == "q" else "lo_kb")
                            add = bias_cols[use[0]](g)
                        nc.scalar.activation(tmp[0:rows, j % 2, :], ps[0:rows, bank_of(kind, m), :], ACT.Identity,
                                             scale=mark, bias=add).then_inc(S[kind, "high_ready"], 1)

            def ffn(r):
                act.wait_ge(logits_shifted, r + 1)
                nc.scalar.activation(pr, lg, ACT.Exp).then_inc(exp_logits, 1)
                for i in range(UNITS * len(FT)):
                    j = UNITS * len(FT) * r + i
                    rows = FT[i % len(FT)][1]
                    act.wait_ge(gate_ready, j + 1)
                    if j >= 2:
                        act.wait_ge(hidden_ready, j - 1)
                    nc.scalar.activation(silu[0:rows, j % 2, :], ps[0:rows, j % 2, :], ACT.Silu).then_inc(silu_done, 1)

            act.wait_ge(loaded["cst"], 16)
            norm(0)
            attention("A")
            norm(1)
            ffn(0)
            norm(2)
            act.wait_ge(biases_ready, 1)
            attention("B")
            norm(3)
            ffn(1)

        @block.vector
        def _(v):
            n_chain = [0]

            def link(ins):
                ins.then_inc(chain, 1)
                n_chain[0] += 1
                v.wait_ge(chain, n_chain[0])

            def norm(r):
                for t in range(NT):
                    if r == 0 and t % TPC == 0:
                        v.wait_ge(loaded["x"], 16 * NC if t else 16 * NC)
                    last = nc.vector.bn_stats(stats[:, t, :], x[:, t, :])
                link(last)
                for t in range(NT):
                    last = nc.vector.bn_aggr(mv[:, t, :], stats[:, t, :])
                link(last)
                nc.vector.tensor_scalar(sc1[:], mv[:, :, 1], EPS, None, ALU.add).then_inc(var_ready, 1)
                v.wait_ge(root_ready, r + 1)
                link(nc.vector.reciprocal(rs[:], sd[:]))
                link(nc.vector.tensor_tensor(sd[:], rs[:], rs[:], ALU.mult))
                link(nc.vector.tensor_tensor(sd[:], sd[:], sc1[:], ALU.mult))
                link(nc.vector.tensor_scalar(sd[:], sd[:], -0.5, 1.5, ALU.mult, ALU.add))
                link(nc.vector.tensor_tensor(rs[:], rs[:], sd[:], ALU.mult))
                for t in range(NT):
                    nc.vector.tensor_scalar(xn[:, t, :], x[:, t, :], mv[:, t, 0:1], rs[:, t:t + 1],
                                            ALU.subtract, ALU.mult).then_inc(norm_ready, 1)
                for c in range(NC):
                    v.wait_ge(high_done, NC * r + c + 1)
                    nc.vector.tensor_tensor(xl[:, c * QC:(c + 1) * QC], ps[:, c, :],
                                            xh[:, c * QC:(c + 1) * QC].bitcast(F32), ALU.subtract).then_inc(parts_done, 1)

            def attention(kind):
                od = orders[kind]
                full, free = S[kind, "ring_full"], S[kind, "ring_free"]
                for ev in od.events:
                    if ev[0] == "evacuate":
                        n = ev[1]
                        last_pair = od.pair_at[n, len(od.key_tiles(n)) - 1]
                        v.wait_ge(S[kind, "product_done"], last_pair + 1)
                        if od.a:
                            link(nc.vector.reciprocal(rinv[:], ps[:, 7, :]))
                            nc.vector.tensor_tensor(ot[:, n % 2, :], ps[:, 6, :], rinv[:], ALU.mult)\
                                .then_inc(S[kind, "evacuated"], 1)
                        else:
                            nc.vector.tensor_copy(o_sb[:], ps[:, 6, :]).then_inc(S[kind, "evacuated"], 1)
                        continue
                    if ev[0] != "ring":
                        continue
                    use = ev[1]
                    m = od.at[use]
                    bank = bank_of(kind, m)
                    v.wait_ge(full, m + 1)
                    if use in od.proj_at:
                        j = od.proj_at[use]
                        v.wait_ge(S[kind, "high_ready"], j + 1)
                        if use[0] == "lat":
                            c = use[1]
                            dst, rows, add = flat[:, c * QC:(c + 1) * QC], P, col("zero")
                        elif use[0] == "k" and od.a:
                            _, g, h, c = use
                            rows, add = KA_ROWS, col("neg_ka", KA_ROWS)
                            dst = kst[0:rows, g % 2, h, c * QC:(c + 1) * QC]
                        elif use[0] == "k":
                            _, g, _, c = use
                            if g and c == 0:
                                v.wait_ge(S[kind, "keys_ready"], 16 * G * g)
                            dst, rows, add = flat[:, c * QC:(c + 1) * QC], P, bias[:, 1, g:g + 1]
                        else:
                            _, n, h = use
                            rows = KA_ROWS if od.a else P
                            add = col("zero", rows) if od.a else bias[:, 0, od.steps[n][0]:od.steps[n][0] + 1]
                            dst = qst[0:rows, n % 2, h, :]
                            if n >= 2:
                                v.wait_ge(S[kind, "scores_ready"], od.tile_at[n - 1, 0, 0])
                        nc.vector.scalar_tensor_tensor(dst, ps[0:rows, bank, :], add, tmp[0:rows, j % 2, :].bitcast(F32),
                                                       ALU.add, ALU.subtract).then_inc(free, 1)
                    elif use[0] == "v":
                        _, g, c = use
                        dst = vst[:, g % 2, c * TPC:(c + 1) * TPC, :]
                        if od.a:
                            nc.vector.tensor_copy(dst, ps[:, bank, :].rearrange("p (t d) -> p t d", d=P)).then_inc(free, 1)
                            continue
                        if g >= 2 and c == 0:
                            v.wait_ge(S[kind, "product_done"], od.last_pair_of_group[g - 2])
                        width = G * DB
                        for q in range(TPC):
                            ins = nc.vector.tensor_tensor(
                                dst[:, q, :].rearrange("p (h r) -> p h r", r=32)[:, :, 0:DB],
                                ps[:, bank, q * width:(q + 1) * width].rearrange("p (h r) -> p h r", r=DB),
                                bv_sb[:, g * width:(g + 1) * width].rearrange("p (h r) -> p h r", r=DB), ALU.add)
                        ins.then_inc(free, 1)
                    elif use[0] == "max":
                        _, n, h, q, k = use
                        first = od.first_key_chunk(n)
                        lo = P * q if (not od.a and k == first) else 0
                        nc.vector.reduce_max(mx[:, h % 2, q, k:k + 1], ps[:, bank, lo:QC], AX.X).then_inc(free, 1)
                        if q == TPC - 1 and k == NC - 1:
                            v.wait_ge(free, m + 1)
                            link(nc.vector.reduce_max(mq[:, n % 2, h, :], mx[:, h % 2, :, first:NC], AX.X))
                            par, at = (h % 2, CA) if od.a else (n % 2, 32 * h + CB)
                            if od.a and (n, h) >= (0, 2):
                                before = ("shift", n, h - 2) if h >= 2 else ("shift", n - 1, h + 2)
                                v.wait_ge(full, od.at[before] + 1)
                            hi = ct[:, par, :, at:at + 1].rearrange("p t a -> p (t a)")
                            lo_part = ct[:, par, :, at + 1:at + 2].rearrange("p t a -> p (t a)")
                            link(nc.vector.tensor_copy(hi, mq[:, n % 2, h, :]))
                            nc.vector.tensor_tensor(lo_part, mq[:, n % 2, h, :], hi.bitcast(F32), ALU.subtract)\
                                .then_inc(S[kind, "shift_parts"], 1)
                    elif use[0] == "shift":
                        _, n, h = use
                        if od.a:
                            nc.vector.tensor_copy(qst[CA:CA + 2, n % 2, h, :], ps[CA:CA + 2, bank, :]).then_inc(free, 1)
                        else:
                            dst = qst[:, n % 2, 0, :]
                            nc.vector.tensor_tensor(dst, ps[:, bank, :], dst.bitcast(F32), ALU.add).then_inc(free, 1)
                    elif use[0] == "sums":
                        n = use[1]
                        link(nc.vector.reciprocal(rinv[:], ps[:, bank, :]))
                        nc.vector.tensor_tensor(ot[:, n % 2, :], o_sb[:], rinv[:], ALU.mult).then_inc(free, 1)
                    elif use[0] == "out":
                        c = od.steps[use[1]][1]
                        xs = x[:, c * TPC:(c + 1) * TPC, :]
                        nc.vector.tensor_tensor(xs, ps[:, bank, :].rearrange("p (t d) -> p t d", d=P), xs, ALU.add)\
                            .then_inc(free, 1)
                v.wait_ge(free, od.uses)
                nc.vector.memset(marker[:, 0:1], 0.0).then_inc(attention_done, 1)
                v.wait_ge(attention_done, 1 if od.a else 2)

            def ffn(r):
                v.wait_ge(logits_ready, r + 1)
                link(nc.vector.tensor_copy(lg, ps[:, 6, 0:NT * E].rearrange("p (t e) -> p t e", e=E)))
                link(nc.vector.reduce_max(lmax[:], lg, AX.X))
                wide = [P, NT, E]

                def spread(a):
                    return a.broadcast_to(wide)

                nc.vector.tensor_tensor(lg, lg, spread(lmax[:].rearrange("p (t a) -> p t a", a=1)), ALU.subtract)\
                    .then_inc(logits_shifted, 1)
                v.wait_ge(exp_logits, r + 1)
                link(nc.vector.reduce_sum(lmax[:], pr, AX.X))
                link(nc.vector.reciprocal(sc1[:], lmax[:]))
                link(nc.vector.tensor_tensor(pr, pr, spread(sc1[:].rearrange("p (t a) -> p t a", a=1)), ALU.mult))
                for t in range(NT):
                    last = nc.vector.max(top[:, t, :], pr[:, t, :])
                link(last)
                for t in range(NT):
                    last = nc.vector.max_index(topi[:, t, :], top[:, t, :], pr[:, t, :])
                link(last)
                link(nc.vector.tensor_copy(topf[:], topi[:, :, 0:2]))
                link(nc.vector.tensor_tensor(lmax[:], top[:, :, 0], top[:, :, 1], ALU.add))
                link(nc.vector.reciprocal(sc1[:], lmax[:]))
                link(nc.vector.tensor_tensor(wtop[:], top[:, :, 0:2],
                                             sc1[:].rearrange("p (t a) -> p t a", a=1).broadcast_to([P, NT, 2]), ALU.mult))
                iota = cst[:, C_IOTA:C_IOTA + E].rearrange("p (a e) -> p a e", a=1).broadcast_to(wide)
                for i, dst in enumerate((cw[:], cw2)):
                    link(nc.vector.tensor_tensor(dst, iota, spread(topf[:, :, i:i + 1]), ALU.is_equal))
                    link(nc.vector.tensor_tensor(dst, dst, spread(wtop[:, :, i:i + 1]), ALU.mult))
                link(nc.vector.tensor_tensor(cw[:], cw[:], cw2, ALU.add))
                units = [(e, c) for e in range(NEXP) for c in range(NC)]

                def add_down(e, c):
                    y = UNITS * r + e * NC + c
                    v.wait_ge(down_ready, y + 1)
                    if e and c == 0:
                        v.wait_ge(added, y)
                    for q in range(TPC):
                        t = c * TPC + q
                        src = ps[:, 4 + y % 2, q * P:(q + 1) * P]
                        if e == 0:
                            ins = nc.vector.tensor_tensor(x[:, t, :], src, x[:, t, :], ALU.add)
                        else:
                            ins = nc.vector.scalar_tensor_tensor(x[:, t, :], src, cw[:, t, e - 1:e], x[:, t, :],
                                                                 ALU.mult, ALU.add)
                    ins.then_inc(added, 1)

                for i, (e, c) in enumerate(units):
                    for f, (_, rows) in enumerate(FT):
                        j = (UNITS * r + i) * len(FT) + f
                        v.wait_ge(silu_done, j + 1)
                        v.wait_ge(up_ready, j + 1)
                        y = UNITS * r + i
                        if f == 0 and y >= 2:
                            v.wait_ge(down_ready, y - 1)
                        nc.vector.tensor_tensor(hid[0:rows, y % 2, f, :], ps[0:rows, 2 + j % 2, :],
                                                silu[0:rows, j % 2, :], ALU.mult).then_inc(hidden_ready, 1)
                        if f == 1 and i:
                            add_down(*units[i - 1])
                add_down(*units[-1])
                v.wait_ge(added, UNITS * (r + 1))

            v.wait_ge(loaded["cst"], 16)
            nc.vector.tensor_copy(identr[:], ident)
            link(nc.vector.tensor_copy(maskr[:], cst[:, C_MT:C_MT + 2 * P].rearrange("p (a n) -> p a n", a=2)))
            norm(0)
            v.wait_ge(filled, 2)
            attention("A")
            norm(1)
            ffn(0)
            norm(2)
            v.wait_ge(loaded["b"], 128)
            v.wait_ge(filled, 3)
            link(nc.vector.tensor_scalar(bias[:, 2, :], bias[:, 0, :], col("lo_qb"), None, ALU.mult))
            nc.vector.tensor_scalar(bias[:, 3, :], bias[:, 1, :], col("lo_kb"), None, ALU.mult).then_inc(biases_ready, 1)
            v.wait_ge(biases_ready, 1)
            link(nc.vector.tensor_scalar(bias[:, 1, :], bias[:, 1, :], col("neg_kb"), None, ALU.add))
            link(nc.vector.tensor_tensor(x[:], x[:], bo_sb[:].rearrange("p (a d) -> p a d", a=1).broadcast_to([P, NT, D]),
                                         ALU.add))
            attention("B")
            norm(3)
            ffn(1)

        @block.tensor
        def _(pe):
            mm = nc.tensor.matmul

            def norm(r):
                for c in range(NC):
                    for q in range(TPC):
                        t = c * TPC + q
                        pe.wait_ge(norm_ready, NT * r + t + 1)
                        last = nc.tensor.transpose(ps[:, c, q * P:(q + 1) * P], xn[:, t, :], ident)
                    last.then_inc(turned, 1)

            def three(dst, wh, wl, xs, start=True, stop=True):
                a, b = xs
                mm(dst, wh, a, start=start, stop=False)
                mm(dst, wh, b, start=False, stop=False)
                return mm(dst, wl, a, start=False, stop=stop)

            def attention(kind):
                od = orders[kind]
                full, free = S[kind, "ring_full"], S[kind, "ring_free"]
                depth = len(ring_banks[kind])
                for ev in od.events:
                    if ev[0] == "scores":
                        _, n, k, h = ev
                        g, c = od.steps[n]
                        t = od.tile_at[n, k, h]
                        if t >= 2:
                            pe.wait_ge(S[kind, "exp_done"], t - 1)
                        if k == 0:
                            pe.wait_ge(free, od.at["shift", n, h if od.a else 0] + 1)
                        rows = KA_ROWS if od.a else P
                        rhs = qst[0:rows, n % 2, h if od.a else 0, :]
                        pair = od.key_tiles(n)[k]
                        flat_bank = ps[:, 2 * (t % 2):2 * (t % 2) + 2, :].rearrange("p b n -> p (b n)")
                        at = 0
                        for kt, w, diagonal in pair:
                            dst = flat_bank[:, at:at + w]
                            last = mm(dst, kst[0:rows, g % 2, h, kt * P:(kt + 1) * P], rhs[:, 0:w],
                                      start=True, stop=not diagonal)
                            if diagonal:
                                last = mm(dst[:, w - P:w], identr[:], maskr[:, 0, :], start=False, stop=True)
                            at += w
                        last.then_inc(S[kind, "scores_ready"], 1)
                    elif ev[0] == "product":
                        _, n, k = ev
                        g, c = od.steps[n]
                        pairs = od.key_tiles(n)
                        kp = od.pair_at[n, k]
                        pe.wait_ge(S[kind, "exp_done"], G * (kp + 1))
                        if k == 0 and n:
                            pe.wait_ge(S[kind, "evacuated"], n)
                        if k == 0:
                            pe.wait_ge(free, od.at["v", g, NC - 1] + 1)
                        at = 0
                        for i, (kt, w, _) in enumerate(pairs[k]):
                            start, stop = k == 0 and i == 0, k == len(pairs) - 1 and i == 1
                            for h in range(G):
                                last = mm(ps[32 * h:32 * h + 32, 6, 0:w], vst[:, g % 2, kt, 32 * h:32 * h + 32],
                                          prob[:, (G * kp + h) % 8, at:at + w], start=start, stop=stop)
                            if od.a:
                                for h in range(G):
                                    last = mm(ps[32 * h:32 * h + 32, 7, 0:w], ones[:],
                                              prob[:, (G * kp + h) % 8, at:at + w], start=start, stop=stop)
                            at += w
                        last.then_inc(S[kind, "product_done"], 1)
                    elif ev[0] == "ring":
                        use = ev[1]
                        m = od.at[use]
                        bank = bank_of(kind, m)
                        if m >= depth:
                            pe.wait_ge(free, m - depth + 1)
                        if use[0] == "lat":
                            c = use[1]
                            xs = (xh[:, c * QC:(c + 1) * QC], xl[:, c * QC:(c + 1) * QC])
                            last = three(ps[:, bank, :], wch[:], wcl[:], xs)
                        elif use[0] == "k" and od.a:
                            _, g, h, c = use
                            pe.wait_ge(free, od.at["lat", NC - 1] + 1)
                            dst, rhs = ps[0:KA_ROWS, bank, :], flat[:, c * QC:(c + 1) * QC]
                            mm(dst, wkh[:, g * G + h, :], rhs, start=True, stop=False)
                            last = mm(dst, wkl[:, g * G + h, :], rhs, start=False, stop=True)
                        elif use[0] == "v":
                            _, g, c = use
                            for q in range(TPC) if od.a else []:
                                lhs = flat[:, c * QC + q * P:c * QC + (q + 1) * P]
                                dst = ps[:, bank, q * P:(q + 1) * P]
                                mm(dst, lhs, wvh[:, g * P:(g + 1) * P], start=True, stop=False)
                                last = mm(dst, lhs, wvl[:, g * P:(g + 1) * P], start=False, stop=True)
                            for q in [] if od.a else range(TPC):
                                s = slice(c * QC + q * P, c * QC + (q + 1) * P)
                                w = slice(g * G * DB, (g + 1) * G * DB)
                                dst = ps[:, bank, q * G * DB:(q + 1) * G * DB]
                                mm(dst, xh[:, s], wvbh[:, w], start=True, stop=False)
                                mm(dst, xl[:, s], wvbh[:, w], start=False, stop=False)
                                last = mm(dst, xh[:, s], wvbl[:, w], start=False, stop=True)
                        elif use[0] == "k":
                            _, g, _, c = use
                            xs = (xh[:, c * QC:(c + 1) * QC], xl[:, c * QC:(c + 1) * QC])
                            last = three(ps[:, bank, :], wkbh[:, g, :], wkbl[:, g, :], xs)
                        elif use[0] == "q":
                            _, n, h = use
                            g, c = od.steps[n]
                            xs = (xh[:, c * QC:(c + 1) * QC], xl[:, c * QC:(c + 1) * QC])
                            if od.a:
                                last = three(ps[0:KA_ROWS, bank, :], wqh[:, g * G + h, :], wql[:, g * G + h, :], xs)
                            else:
                                last = three(ps[:, bank, :], wqbh[:, g, :], wqbl[:, g, :], xs)
                        elif use[0] == "max":
                            _, n, h, q, k = use
                            g, c = od.steps[n]
                            if q == 0 and k == od.first_key_chunk(n):
                                pe.wait_ge(free, od.at["q", n, h if od.a else 0] + 1)
                                if od.a:
                                    pe.wait_ge(free, od.at["k", g, G - 1, NC - 1] + 1)
                                else:
                                    pe.wait_ge(S[kind, "keys_ready"], 16 * G * (g + 1))
                            rows = CA if od.a else P
                            diagonal = not od.a and k == c
                            lo = P * q if diagonal else 0
                            lhs = qst[0:rows, n % 2, h if od.a else 0, q * P:(q + 1) * P]
                            last = mm(ps[:, bank, lo:QC], lhs, kst[0:rows, g % 2, h, k * QC + lo:(k + 1) * QC],
                                      start=True, stop=not diagonal)
                            if diagonal:
                                last = mm(ps[:, bank, lo:lo + P], identr[:], maskr[:, 1, :], start=False, stop=True)
                        elif use[0] == "shift":
                            _, n, h = use
                            if od.a:
                                pe.wait_ge(S[kind, "shift_parts"], G * n + h + 1)
                                rows, par = KA_ROWS, h % 2
                            else:
                                pe.wait_ge(S[kind, "shift_parts"], G * (n + 1))
                                rows, par = P, n % 2
                            for q in range(TPC):
                                last = mm(ps[0:rows, bank, q * P:(q + 1) * P], ct[:, par, q, 0:rows], identr[:],
                                          start=True, stop=True)
                        elif use[0] == "sums":
                            n = use[1]
                            pe.wait_ge(S[kind, "evacuated"], n + 1)
                            last = mm(ps[:, bank, :], sel, o_sb[:], start=True, stop=True)
                        elif use[0] == "out":
                            n = use[1]
                            g, c = od.steps[n]
                            if od.a:
                                pe.wait_ge(S[kind, "evacuated"], n + 1)
                            else:
                                pe.wait_ge(free, od.at["sums", n] + 1)
                            for q in range(TPC):
                                last = mm(ps[:, bank, q * P:(q + 1) * P], ot[:, n % 2, q * P:(q + 1) * P],
                                          (wo_a_sb if od.a else wo_b_sb)[:, g, :], start=True, stop=True)
                        last.then_inc(full, 1)

            def ffn(r):
                for t in range(NT):
                    s = slice(t * P, (t + 1) * P)
                    dst = ps[:, 6, t * E:(t + 1) * E]
                    mm(dst, xh[:, s], gwh[:], start=True, stop=False)
                    mm(dst, xl[:, s], gwh[:], start=False, stop=False)
                    mm(dst, xh[:, s], gwl[:], start=False, stop=False)
                    last = mm(dst, xl[:, s], gwl[:], start=False, stop=True)
                last.then_inc(logits_ready, 1)
                units = [(e, c) for e in range(NEXP) for c in range(NC)]

                def down(i):
                    e, c = units[i]
                    n, y = NEXP * r + e, UNITS * r + i
                    pe.wait_ge(hidden_ready, (y + 1) * len(FT))
                    if y >= 2:
                        pe.wait_ge(added, y - 1)
                    for q in range(TPC):
                        for f, (_, rows) in enumerate(FT):
                            last = mm(ps[:, 4 + y % 2, q * P:(q + 1) * P], hid[0:rows, y % 2, f, q * P:(q + 1) * P],
                                      wd[0:rows, n % 2, f, :], start=f == 0, stop=f == len(FT) - 1)
                    last.then_inc(down_ready, 1)

                for i, (e, c) in enumerate(units):
                    n = NEXP * r + e
                    if c == 0:
                        pe.wait_ge(gu_split, 2 * (n + 1))
                    xs = (xh[:, c * QC:(c + 1) * QC], xl[:, c * QC:(c + 1) * QC])
                    for f, (at, rows) in enumerate(FT):
                        j = (UNITS * r + i) * len(FT) + f
                        if j >= 2:
                            pe.wait_ge(silu_done, j - 1)
                        three(ps[0:rows, j % 2, :], wguh[:, n % 2, at:at + rows], wgul[:, n % 2, at:at + rows], xs)\
                            .then_inc(gate_ready, 1)
                        if j >= 2:
                            pe.wait_ge(hidden_ready, j - 1)
                        three(ps[0:rows, 2 + j % 2, :], wguh[:, n % 2, I + at:I + at + rows],
                              wgul[:, n % 2, I + at:I + at + rows], xs).then_inc(up_ready, 1)
                        if f == 0 and i:
                            down(i - 1)
                down(len(units) - 1)

            pe.wait_ge(loaded["cst"], 16)
            norm(0)
            pe.wait_ge(parts_done, NC)
            pe.wait_ge(filled, 2)
            pe.wait_ge(weights_split, split_count("gw"))
            attention("A")
            norm(1)
            pe.wait_ge(parts_done, 2 * NC)
            ffn(0)
            norm(2)
            pe.wait_ge(parts_done, 3 * NC)
            pe.wait_ge(weights_split, split_count("wvb"))
            pe.wait_ge(filled, 5)
            attention("B")
            norm(3)
            pe.wait_ge(parts_done, 4 * NC)
            ffn(1)


def stack_heads(w, heads, width, parts, pitch):
    w = w.reshape(w.shape[0], heads, width)
    zero = np.zeros((w.shape[0], heads, pitch - parts * width), w.dtype)
    return np.concatenate([w] * parts + [zero], axis=2)


def kernel(L0_attn_a_x, L0_attn_a_Wq, L0_attn_a_Wkv_down, L0_attn_a_Wk_up, L0_attn_a_Wv_up, L0_attn_a_Wo,
           L0_attn_b_w_qkv, L0_attn_b_b_qkv, L0_attn_b_w_out, L0_attn_b_b_out, L0_ffn_gate_w,
           L0_ffn_base_wgu, L0_ffn_base_wd, L0_ffn_exp_wgu, L0_ffn_exp_wd):
    import concourse.bacc as bacc
    from concourse.bass_utils import run_bass_kernel_spmd

    f = lambda a: np.asarray(a)
    x = f(L0_attn_a_x).reshape(T, D)
    wqkv, bqkv = f(L0_attn_b_w_qkv), f(L0_attn_b_b_qkv)
    b3 = bqkv.reshape(3, 1, D)
    bias_cols = lambda b: stack_heads(b, HB, DB, 3, 32).reshape(GB, P).T
    wob = f(L0_attn_b_w_out).reshape(HB, DB, D)
    wob = np.concatenate([wob, np.zeros((HB, 32 - DB, D), wob.dtype)], axis=1)
    wk = f(L0_attn_a_Wk_up).T
    wv = f(L0_attn_a_Wv_up).T
    kv = f(L0_attn_a_Wkv_down).T
    arrays = {
        "x": x,
        "wq_a": stack_heads(f(L0_attn_a_Wq).T, HA, DA, 3, KA_ROWS),
        "wkv_a": np.concatenate([kv, kv], axis=1),
        "wk_a": stack_heads(np.concatenate([wk, wk], axis=0), HA, DA, 3, KA_ROWS),
        "wv_a": np.concatenate([wv, wv], axis=0),
        "wo_a": f(L0_attn_a_Wo).T.reshape(GA, P, D).transpose(1, 0, 2),
        "wq_b": stack_heads(wqkv[:, 0:D], HB, DB, 3, 32).reshape(D, GB, P),
        "wk_b": stack_heads(wqkv[:, D:2 * D], HB, DB, 3, 32).reshape(D, GB, P),
        "wv_b": wqkv[:, 2 * D:3 * D],
        "bq_b": bias_cols(b3[0]),
        "bk_b": bias_cols(b3[1]),
        "bv_b": b3[2],
        "wo_b": wob.reshape(GB, P, D).transpose(1, 0, 2),
        "bo_b": f(L0_attn_b_b_out).reshape(1, D),
        "gate_w": f(L0_ffn_gate_w),
        "base_wgu": f(L0_ffn_base_wgu),
        "base_wd": f(L0_ffn_base_wd),
        "exp_wgu": f(L0_ffn_exp_wgu),
        "exp_wd": f(L0_ffn_exp_wd),
        "consts": constants(),
    }
    arrays = {n: np.ascontiguousarray(a) for n, a in arrays.items()}
    nc = bacc.Bacc("TRN2", target_bir_lowering=False, num_devices=1)
    args = [nc.dram_tensor("in_" + n, a.shape, mybir.dt.from_np(a.dtype), kind="ExternalInput").ap()
            for n, a in arrays.items()]
    out = nc.dram_tensor("out_x", (T, D), F32, kind="ExternalOutput").ap()
    build(nc, *args, out)
    r = run_bass_kernel_spmd(nc, [{"in_" + n: a for n, a in arrays.items()}], core_ids=[0])
    return r.results[0]["out_x"].reshape(1, T, D)
```

```python
import numpy as np
import concourse.bass as bass
from concourse import mybir
from contextlib import ExitStack

F32 = mybir.dt.float32
F32R = mybir.dt.float32r
U32 = mybir.dt.uint32
ALU = mybir.AluOpType
ACT = mybir.ActivationFunctionType
AX = mybir.AxisListType

P = 128
T, D = 2048, 128
NT = T // P
QC = 512
NC = T // QC
TPC = QC // P
G = 4
HA, DA, RANK = 8, 32, 64
HB, DB = 16, 8
GA, GB = HA // G, HB // G
E, I = 8, 352
FT = [(0, 128), (128, 128), (256, 96)]
EPS = 1e-5
MASKED = -1e38
SA = 32
CA = 3 * SA
KA_ROWS = CA + 2
CB = 3 * DB
BANKS = 3
RING = {"A": [3, 4, 5], "B": [3, 4, 5, 7]}
VALUES, ONES = 6, 7
START_BANKS = [0, 1, 2, 7]
SLOTS = 18

C_ID, C_SEL, C_COL = 0, 128, 256
COLS = ["lo_qa", "lo_ka", "lo_lat", "neg_ka", "lo_qb", "lo_kb", "neg_kb", "zero"]
C_IOTA = C_COL + len(COLS)
C_ALL = C_IOTA + E


def constants():
    c = np.zeros((P, C_ALL), np.float32)
    r = np.arange(P)
    c[:, C_ID:C_ID + P] = np.eye(P)
    c[32 * (r // 32) + DB, C_SEL + r] = 1.0
    cols = {
        "lo_qa": (r // SA == 1),
        "lo_ka": (r // SA == 2),
        "lo_lat": (r >= RANK),
        "neg_ka": -1.0 * ((r == CA) | (r == CA + 1)),
        "lo_qb": (r % 32 // DB == 1),
        "lo_kb": (r % 32 // DB == 2),
        "neg_kb": -1.0 * ((r % 32 == CB) | (r % 32 == CB + 1)),
        "zero": 0 * r,
    }
    for i, n in enumerate(COLS):
        c[:, C_COL + i] = cols[n]
    c[:, C_IOTA:C_IOTA + E] = np.arange(E)[None, :]
    return c


def diagonal_masks():
    r = np.arange(P)
    return np.stack([np.where(r[None, :] > r[:, None], MASKED, 0),
                     np.where(r[None, :] < r[:, None], MASKED, 0)], axis=1).astype(np.float32)


class Order:

    LAG = 0.25

    def __init__(self, kind):
        self.kind = kind
        self.a = kind == "A"
        self.groups = GA if self.a else GB
        if self.a:
            self.steps = [(g, c) for g in range(GA) for c in range(NC)]
        else:
            self.steps = [(g, c) for g in range(GB) for c in (range(NC) if g % 2 else reversed(range(NC)))]
        self.ahead = 1 if self.a else 2
        self.events, self.at, self.uses = [], {}, 0
        self.tiles, self.tile_at, self.projections = 0, {}, 0
        self.key_count, self.key_at = 0, {}
        self.proj_at, self.last_tile_of_group, self.last_key_of_group = {}, {}, {}
        self.tensor, self.vector, self.freed, self.ready = 0.0, 0.0, [], {}
        self.build()

    def key_tiles(self, n):
        g, c = self.steps[n]
        if self.a:
            return [(k, QC, False) for k in range(NT)]
        ks = [(c * TPC + d, (d + 1) * P, True) for d in reversed(range(TPC))]
        return ks + [(k, QC, False) for k in range((c + 1) * TPC, NT)]

    def first_key_chunk(self, n):
        return 0 if self.a else self.steps[n][1]

    def width(self, n, q, k):
        return QC - P * q if not self.a and k == self.first_key_chunk(n) else QC

    def costs(self, use):
        kind = use[0]
        if kind == "max":
            w = self.width(use[1], *use[3:])
            return 0.0004 * w + (0.06 if w < QC or not self.a else 0), 0.06 + w / 960
        return {"q": (0.65, 0.7), "k": (0.45 if self.a else 0.65, 0.7), "lat": (0.65, 0.7), "v": (0.4, 0.6),
                "shift": (0.3, 0.65), "sums": (0.9, 1.3), "out": (0.9, 0.65), "turn": (0.3, 0.65)}[kind]

    def ring(self, *use):
        bank_free = self.freed[self.uses - len(RING[self.kind])] if self.uses >= len(RING[self.kind]) else 0
        pe, dve = self.costs(use)
        self.tensor = max(self.tensor, bank_free) + pe
        wait = 1.0 if use[0] in ("q", "k", "lat", "turn") else self.LAG
        self.vector = max(self.vector, self.tensor + wait) + dve
        self.freed.append(self.vector + self.LAG)
        self.ready[use] = self.vector + self.LAG
        if use[0] == "max" and use[3] == TPC - 1 and use[4] == NC - 1:
            self.vector += 0.4
            self.ready["parts", use[1], use[2]] = self.vector + 3 * self.LAG
        self.at[use] = self.uses
        self.uses += 1
        if use[0] in ("q", "k", "lat"):
            self.proj_at[use] = self.projections
            self.projections += 1
        self.events.append(("ring", use))

    def for_group(self, g):
        heads = range(G) if self.a else [0]
        return [("k", g, h, c) for c in range(NC) for h in heads] + [("v", g, c) for c in range(NC)]

    def for_queries(self, n):
        kcs = range(self.first_key_chunk(n), NC)
        out = [("q", n, h) for h in (range(G) if self.a else [0])]
        for h in range(G):
            out += [("max", n, h, q, k) for q in range(TPC) for k in kcs]
            if self.a or h == G - 1:
                out.append(("shift", n, h if self.a else 0))
        return out

    def when(self, use):
        if use[0] == "max":
            _, n, h, _, _ = use
            keys = self.ready.get(("k", self.steps[n][0], G - 1 if self.a else 0, NC - 1), 0)
            return max(self.ready[("q", n, h if self.a else 0)], keys + (0 if self.a else 4))
        if use[0] == "shift":
            return self.ready["parts", use[1], use[2] if self.a else G - 1]
        return 0

    def prepare(self, todo):
        for _ in range(3):
            depth = len(RING[self.kind])
            if self.uses >= depth and self.freed[self.uses - depth] > self.tensor:
                return
            use = self.next_of(todo)
            if use is None:
                return
            self.ring(*use)

    def next_of(self, todo, force=False):
        if not todo:
            return None
        if force or self.when(todo[0]) <= self.tensor:
            return todo.pop(0)
        if todo[0][0] == "shift" and len(todo) > 1:
            use = todo[1]
            if (use[0] == "q" or use[0] == "max" and use[3] < TPC - 1) and self.when(use) <= self.tensor:
                return todo.pop(1)
        return None

    def build(self):
        if self.a:
            for c in range(NC):
                self.ring("lat", c)
        for use in self.for_group(0) + self.for_queries(0):
            self.ring(*use)
        last = len(self.steps) - 1
        planned = 0
        todo, late = [], []
        for n, (g, c) in enumerate(self.steps):
            keys = self.key_tiles(n)
            if n % NC == 0 and g + 1 < self.groups:
                todo = self.for_group(g + 1) + todo
            while planned < min(last, n + self.ahead):
                planned += 1
                todo += self.for_queries(planned)
            for u in range(G * len(keys)):
                k, h = divmod(u, G)
                self.events.append(("scores", n, k, h))
                self.tensor += 0.22 * keys[k][1] / QC + (0.06 if keys[k][2] else 0)
                self.tile_at[n, k, h] = self.tiles
                self.tiles += 1
                if h == 0:
                    self.key_at[n, k] = self.key_count
                    self.key_count += 1
                for item in [x for x in late if x[0] <= u]:
                    late.remove(item)
                    self.do(item[1], late, u)
                self.prepare(todo)
                self.products(n, k, h, late, u)
                self.prepare(todo)
            while todo and any(x[0] in ("q", "max", "shift") and x[1] == n + 1 for x in todo):
                self.ring(*(self.next_of(todo) or self.next_of(todo, force=True)))
            late = [(max(0, at - G * len(keys)), ev) for at, ev in late]
            self.last_tile_of_group[g] = self.tiles
            self.last_key_of_group[g] = self.key_count
        keys = len(self.key_tiles(last))
        self.values((last, keys - 1), late, 0)
        if self.a:
            self.ones(self.key_count // 2 - 2)
            self.ones(self.key_count // 2 - 1)
            late.append((0, ("weigh", last)))
        while late:
            self.do(late.pop(0)[1], late, 0)

    def do(self, ev, late, u):
        if ev[0] in ("sums", "out", "turn"):
            self.ring(*ev)
        else:
            self.events.append(ev)
            self.vector += {"weigh": 1.3, "norm_a": 1.5, "norm_b": 1.5}.get(ev[0], 0)
        n = ev[1]
        follow = {"weigh": (5, ("out", n)), "sums": (6, ("out", n))}.get(ev[0])
        if ev[0] == "out" and self.steps[n][0] == self.groups - 1:
            follow = (2, ("norm_a", self.steps[n][1]))
        if ev[0] == "norm_a":
            follow = (3, ("norm_b", n))
        if ev[0] == "norm_b":
            follow = (4, ("turn", n))
        if follow:
            late.append((u + follow[0], follow[1]))

    def products(self, n, k, h, late, u):
        at = (n, k - 1) if k else (n - 1, len(self.key_tiles(n - 1)) - 1)
        if h == 1 and at[0] >= 0:
            self.values(at, late, u)
        count = self.key_count - 1
        if self.a and h == 0 and count % 2 == 0 and count >= 4:
            pair = (count - 4) // 2
            self.ones(pair)
            if pair % (NT // 2) == NT // 2 - 1:
                late.append((u + 1, ("weigh", pair // (NT // 2))))

    def values(self, at, late, u):
        self.events.append(("values", *at))
        self.tensor += max(0.15, 1.0 * self.key_tiles(at[0])[at[1]][1] / QC)
        if at[1] == len(self.key_tiles(at[0])) - 1:
            self.events.append(("evacuate", at[0]))
            if not self.a:
                late.append((u + 3, ("sums", at[0])))

    def ones(self, pair):
        self.events.append(("ones", pair))
        self.tensor += 1.0


def build(nc, x_in, wq_a, wkv_a, wk_a, wv_a, wo_a, wq_b, wk_b, wv_b, bq_b, bk_b, bv_b, wo_b, bo_b,
          gate_w, base_wgu, base_wd, exp_wgu, exp_wd, consts, masks, out):
    orders = {"A": Order("A"), "B": Order("B")}
    ctx = ExitStack()
    with ctx:
        def sb(name, shape, dt=F32):
            return ctx.enter_context(nc.sbuf_tensor(name, shape, dt))

        def sem(name):
            return ctx.enter_context(nc.semaphore(name))

        cst = sb("cst", [P, C_ALL])
        ident = cst[:, C_ID:C_ID + P]
        sel = cst[:, C_SEL:C_SEL + P]
        identr = sb("identr", [P, P], F32R)
        maskr = sb("maskr", [P, 2, P], F32R)
        ones = sb("ones", [P, 32])
        x = sb("x", [P, NT, D])
        xh = sb("xh", [P, T], F32R)
        xl = sb("xl", [P, T], F32R)
        kst = sb("kst", [P, 2, G, T], F32R)
        qst = sb("qst", [P, 2, G, QC], F32R)
        vst = sb("vst", [P, 2, NT, P])
        prob = sb("prob", [P, SLOTS, QC])
        tmp = sb("tmp", [P, 2, QC], F32R)
        flat = sb("flat", [P, T], F32R)
        mx = sb("mx", [P, 2, TPC, NC])
        mq = sb("mq", [P, 2, G, TPC])
        ct = sb("ct", [P, 2, TPC, P], F32R)
        o_sb = sb("o_sb", [P, QC])
        rinv = sb("rinv", [P, QC])
        ot = sb("ot", [P, QC])
        spare = prob[:].rearrange("p a n -> p (a n)")

        def in_spare(at, *shape):
            n = int(np.prod(shape))
            names = "abc"[:len(shape)]
            a = spare[:, at:at + n]
            if len(shape) == 1:
                return a
            return a.rearrange(f"p ({' '.join(names)}) -> p {' '.join(names)}", **dict(zip(names, shape)))

        xn = sb("xn", [P, 2, TPC, D])

        stats = sb("stats", [P, NT, 6])
        mv = sb("mv", [P, NT, 2])
        marker = sb("marker", [P, 2])
        ve = sb("ve", [P, NT])
        rs = sb("rs", [P, NT])
        newton = sb("newton", [P, TPC])
        minus_half = sb("minus_half", [P, TPC])
        mask_raw = in_spare(3072, 2, P)
        wq_raw, wqh, wql = in_spare(0, HA, KA_ROWS), sb("wqh", [P, HA, KA_ROWS], F32R), sb("wql", [P, HA, KA_ROWS], F32R)
        wk_raw, wkh, wkl = in_spare(1024, HA, KA_ROWS), sb("wkh", [P, HA, KA_ROWS], F32R), sb("wkl", [P, HA, KA_ROWS], F32R)
        wv_raw, wvh, wvl = in_spare(2048, HA * DA), sb("wvh", [P, HA * DA], F32R), sb("wvl", [P, HA * DA], F32R)
        wc_raw, wch, wcl = in_spare(2048 + HA * DA, P), sb("wch", [P, P], F32R), sb("wcl", [P, P], F32R)
        wqb_raw, wkb_raw, wvb_raw = (a.rearrange("p (g n) -> p g n", n=P) for a in (o_sb[:], rinv[:], ot[:]))
        wvb_raw = wvb_raw[:, 0, :]
        wqbh, wqbl, wkbh, wkbl = (w[:].rearrange("p h n -> p (h n)")[:, 0:GB * P].rearrange("p (g n) -> p g n", n=P)
                                  for w in (wqh, wql, wkh, wkl))
        wvbh, wvbl = wch[:], wcl[:]
        wo_sb = sb("wo_sb", [P, GB, D])
        bias = sb("bias", [P, 4, GB])
        bv_sb = sb("bv_sb", [P, D])
        bo_sb = in_spare(16 * QC, D)
        gw_raw, gwh, gwl = sb("gw_raw", [P, E]), sb("gwh", [P, E], F32R), sb("gwl", [P, E], F32R)
        wgu = in_spare(9 * QC, 2, 2 * I)
        queries_flat = qst[:].rearrange("p a h n -> p (a h n)")
        wguh, wgul = (queries_flat[:, i * 4 * I:(i + 1) * 4 * I].rearrange("p (a n) -> p a n", a=2) for i in range(2))
        wd = in_spare(16 * QC + 2 * P, 2, len(FT), D)
        silu = in_spare(0, 2, QC)
        hid = in_spare(2 * QC, 2, len(FT), QC)
        lg, pr, top, cw2 = (in_spare(8 * QC + i * P, NT, E) for i in range(4))
        lmax = sb("lmax", [P, NT])
        lrecip = sb("lrecip", [P, NT])
        topi = in_spare(16 * QC + P, NT, 8).bitcast(U32)
        topf = sb("topf", [P, NT, 2])
        wtop = sb("wtop", [P, NT, 2])
        cw = sb("cw", [P, NT, E])

        ps = ctx.enter_context(nc.psum_tensor("ps", [P, 8, QC], F32))

        def bank_of(kind, m):
            return RING[kind][m % len(RING[kind])]

        def q_slot(od, n, h):
            return qst[:, n % 2, h if od.a else n // 2 % 2, :]

        Q_STEPS = {"A": 2, "B": 4}

        def col(name, rows=P):
            i = C_COL + COLS.index(name)
            return cst[0:rows, i:i + 1]

        loaded = {n: sem("loaded_" + n) for n in ("cst", "qa", "ca", "ka", "va", "small", "b", "masks")}
        loaded["x"] = [sem(f"loaded_x{c}") for c in range(NC)]
        weights_split = sem("weights_split")
        filled = sem("filled")
        S = {}
        for kind in "AB":
            for n in ("scores_ready", "exp_done", "values_done", "ring_full", "ring_free",
                      "high_ready", "evacuated", "shift_parts", "keys_ready"):
                S[kind, n] = sem(n + "_" + kind)
        chain = sem("vector_chain")
        pair_summed, ones_done, weighed = sem("pair_summed"), sem("ones_done"), sem("weighed")
        var_ready, root_ready = sem("var_ready"), sem("root_ready")
        norm_ready, turned, high_done, parts_done = sem("norm_ready"), sem("turned"), sem("high_done"), sem("parts_done")
        logits_taken = sem("logits_taken")
        logits_ready, logits_shifted, exp_logits = sem("logits_ready"), sem("logits_shifted"), sem("exp_logits")
        gu_loaded = [sem("gu_loaded0"), sem("gu_loaded1")]
        gu_split, gate_ready, up_ready, silu_done, hidden_ready, down_ready, added = (
            sem(n) for n in ("gu_split", "gate_ready", "up_ready", "silu_done", "hidden_ready", "down_ready", "added"))
        stored = sem("stored")
        attention_done, biases_ready = sem("attention_done"), sem("biases_ready")

        NEXP = E + 1
        UNITS = NEXP * NC
        SPLITS = ["wc", "wq", "wk", "wv", "gw", "wqb", "wkb", "wvb"]

        def split_count(name):
            return 2 * (SPLITS.index(name) + 1)

        def wait_parts(eng, r, c):
            if r % 2 == 0:
                eng.wait_ge(parts_done, NC * (r // 2) + c + 1)
            else:
                kind = "AB"[r // 2]
                eng.wait_ge(S[kind, "ring_free"], orders[kind].at["turn", c] + 1)

        block = ctx.enter_context(nc.Block())

        @block.sync
        def _(sp):
            sp.dma_start(cst[:], consts).then_inc(loaded["cst"], 16)
            sp.dma_start(mask_raw, masks).then_inc(loaded["masks"], 16)
            for c in range(NC):
                sp.dma_start(x[:, c * TPC:(c + 1) * TPC, :],
                             x_in[c * QC:(c + 1) * QC, :].rearrange("(t p) d -> p t d", p=P)).then_inc(loaded["x"][c], 16)
            sp.dma_start(wc_raw, wkv_a).then_inc(loaded["ca"], 16)
            sp.dma_start(wq_raw, wq_a).then_inc(loaded["qa"], 16)
            sp.dma_start(wk_raw, wk_a).then_inc(loaded["ka"], 16)
            sp.dma_start(wv_raw, wv_a).then_inc(loaded["va"], 16)
            sp.dma_start(wo_sb[:, 0:GA, :], wo_a).then_inc(loaded["small"], 16)
            sp.dma_start(gw_raw[:], gate_w).then_inc(loaded["small"], 16)
            sp.wait_ge(attention_done, 1)
            for dst, src in ((wqb_raw, wq_b), (wkb_raw, wk_b), (wvb_raw, wv_b), (wo_sb[:], wo_b),
                             (bias[:, 0, :], bq_b), (bias[:, 1, :], bk_b)):
                sp.dma_start(dst, src).then_inc(loaded["b"], 16)
            sp.dma_start(bv_sb[:], bv_b.broadcast_to([P, D])).then_inc(loaded["b"], 16)
            sp.dma_start(bo_sb, bo_b.broadcast_to([P, D])).then_inc(loaded["b"], 16)

            def load_expert(n, gu, down):
                par = n % 2
                if n >= 2:
                    sp.wait_ge(gu_split, 2 * (n - 1))
                    sp.wait_ge(down_ready, NC * (n - 1))
                sp.dma_start(wgu[:, par, :], gu).then_inc(gu_loaded[par], 16)
                sp.dma_start(wd[:, par, 0:2, :], down[0:256, :].rearrange("(f p) d -> p f d", p=P)).then_inc(gu_loaded[par], 16)
                sp.dma_start(wd[0:96, par, 2, :], down[256:I, :]).then_inc(gu_loaded[par], 16)

            def load_experts(r):
                load_expert(NEXP * r, base_wgu, base_wd)
                for e in range(E):
                    load_expert(NEXP * r + e + 1, exp_wgu[e], exp_wd[e])

            load_experts(0)
            od = orders["B"]
            for g in range(GB):
                sp.wait_ge(S["B", "ring_free"], od.at["k", g, 0, NC - 1] + 1)
                if g == 0:
                    sp.wait_ge(filled, 6)
                if g >= 2:
                    sp.wait_ge(S["B", "scores_ready"], od.last_tile_of_group[g - 2])
                for h in range(G):
                    sp.dma_start(kst[32 * h:32 * h + 32, g % 2, h, :].bitcast(F32),
                                 flat[32 * h:32 * h + 32, :].bitcast(F32)).then_inc(S["B", "keys_ready"], 16)
            sp.wait_ge(attention_done, 2)
            load_experts(1)
            for c in range(NC):
                sp.wait_ge(added, NEXP * NC + (NEXP - 1) * NC + c + 1)
                sp.dma_start(out[c * QC:(c + 1) * QC, :].rearrange("(t p) d -> p t d", p=P),
                             x[:, c * TPC:(c + 1) * TPC, :]).then_inc(stored, 16)
            sp.wait_ge(stored, 16 * NC)

        @block.gpsimd
        def _(pool):
            n_split = [0]

            def split(hi, lo, raw):
                nc.gpsimd.tensor_copy(hi, raw).then_inc(weights_split, 1)
                n_split[0] += 1
                pool.wait_ge(weights_split, n_split[0])
                nc.gpsimd.tensor_tensor(lo, raw, hi.bitcast(F32), ALU.subtract).then_inc(weights_split, 1)
                n_split[0] += 1

            def power(i):
                c = i % NC
                pool.wait_ge(var_ready, i + 1)
                t = slice(c * TPC, (c + 1) * TPC)
                nc.gpsimd.tensor_tensor(rs[:, t], ve[:, t], minus_half[:], ALU.pow).then_inc(root_ready, 1)

            def attention(kind, r):
                od = orders[kind]
                for ev in od.events:
                    if ev[0] == "norm_a":
                        power(NC * r + ev[1])
                    elif ev[0] == "scores" and od.a and od.key_at[ev[1], ev[2]] % 2:
                        _, n, k, h = ev
                        key = od.key_at[n, k]
                        pool.wait_ge(S["A", "exp_done"], G * key + h + 1)
                        pool.wait_ge(S["A", "values_done"], key)
                        first, second = prob[:, (G * (key - 1) + h) % SLOTS, :], prob[:, (G * key + h) % SLOTS, :]
                        nc.gpsimd.tensor_tensor(first, first, second, ALU.add).then_inc(pair_summed, 1)

            nc.gpsimd.memset(minus_half[:], -0.5).then_inc(filled, 1)
            nc.gpsimd.memset(ones[:], 1.0).then_inc(filled, 1)
            nc.gpsimd.memset(ct[:].bitcast(F32), 0.0).then_inc(filled, 1)
            pool.wait_ge(filled, 1)
            for c in range(NC):
                power(c)
            pool.wait_ge(loaded["ca"], 16)
            split(wch[:], wcl[:], wc_raw)
            pool.wait_ge(loaded["qa"], 16)
            split(wqh[:], wql[:], wq_raw)
            pool.wait_ge(loaded["ka"], 16)
            split(wkh[:], wkl[:], wk_raw)
            pool.wait_ge(loaded["va"], 16)
            split(wvh[:], wvl[:], wv_raw)
            pool.wait_ge(loaded["small"], 32)
            split(gwh[:], gwl[:], gw_raw[:])

            def split_expert(n):
                par = n % 2
                pool.wait_ge(gu_loaded[par], 48 * (n // 2 + 1))
                if n >= 2:
                    pool.wait_ge(up_ready, len(FT) * NC * (n - 1))
                nc.gpsimd.tensor_copy(wguh[:, par, :], wgu[:, par, :]).then_inc(gu_split, 1)
                pool.wait_ge(gu_split, 2 * n + 1)
                nc.gpsimd.tensor_tensor(wgul[:, par, :], wgu[:, par, :], wguh[:, par, :].bitcast(F32),
                                        ALU.subtract).then_inc(gu_split, 1)

            attention("A", 1)
            pool.wait_ge(attention_done, 1)
            for n in range(2):
                split_expert(n)
            nc.gpsimd.memset(ct[:].bitcast(F32), 0.0).then_inc(filled, 1)
            nc.gpsimd.memset(vst[:], 1.0).then_inc(filled, 1)
            nc.gpsimd.memset(kst[:].bitcast(F32), 0.0).then_inc(filled, 1)
            pool.wait_ge(loaded["b"], 128)
            split(wqbh[:], wqbl[:], wqb_raw)
            split(wkbh[:], wkbl[:], wkb_raw)
            split(wvbh[:], wvbl[:], wvb_raw)
            for n in range(2, NEXP):
                split_expert(n)
            for c in range(NC):
                power(2 * NC + c)
            attention("B", 3)
            pool.wait_ge(attention_done, 2)
            for n in range(NEXP, 2 * NEXP):
                split_expert(n)

        @block.scalar
        def _(act):
            def high_part(i, bank):
                c = i % NC
                nc.scalar.activation(xh[:, c * QC:(c + 1) * QC], ps[:, bank, :], ACT.Identity).then_inc(high_done, 1)

            def attention(kind, r):
                od = orders[kind]
                bias_cols = {"q": lambda g: bias[:, 2, g:g + 1], "k": lambda g: bias[:, 3, g:g + 1]}
                for ev in od.events:
                    if ev[0] == "scores":
                        _, n, k, h = ev
                        t = od.tile_at[n, k, h]
                        w = od.key_tiles(n)[k][1]
                        act.wait_ge(S[kind, "scores_ready"], t + 1)
                        if t >= SLOTS:
                            key = (t - SLOTS) // G
                            if od.a:
                                act.wait_ge(ones_done, key // 2 + 1)
                            else:
                                act.wait_ge(S[kind, "values_done"], key + 1)
                        nc.scalar.activation(prob[:, t % SLOTS, 0:w], ps[:, t % BANKS, 0:w], ACT.Exp,
                                             scale=float((DA if od.a else DB) ** -0.5)).then_inc(S[kind, "exp_done"], 1)
                    elif ev[0] == "evacuate":
                        n = ev[1]
                        act.wait_ge(S[kind, "values_done"], od.key_at[n, len(od.key_tiles(n)) - 1] + 1)
                        if n and od.a:
                            act.wait_ge(weighed, n)
                        elif n:
                            act.wait_ge(S[kind, "ring_free"], od.at["sums", n - 1] + 1)
                        nc.scalar.activation(o_sb[:], ps[:, VALUES, :], ACT.Identity).then_inc(S[kind, "evacuated"], 1)
                    elif ev[0] == "ring" and ev[1][0] == "turn":
                        act.wait_ge(S[kind, "ring_full"], od.at[ev[1]] + 1)
                        high_part(NC * r + ev[1][1], bank_of(kind, od.at[ev[1]]))
                    elif ev[0] == "ring" and ev[1] in od.proj_at:
                        use = ev[1]
                        m, j = od.at[use], od.proj_at[use]
                        rows = P if (use[0] == "lat" or not od.a) else KA_ROWS
                        act.wait_ge(S[kind, "ring_full"], m + 1)
                        if j >= 2:
                            before = [u for u, i in od.proj_at.items() if i == j - 2][0]
                            act.wait_ge(S[kind, "ring_free"], od.at[before] + 1)
                        if od.a:
                            mark = col({"q": "lo_qa", "k": "lo_ka", "lat": "lo_lat"}[use[0]], rows)
                            add = 0.0
                        else:
                            g = od.steps[use[1]][0] if use[0] == "q" else use[1]
                            mark = col("lo_qb" if use[0] == "q" else "lo_kb")
                            add = bias_cols[use[0]](g)
                        nc.scalar.activation(tmp[0:rows, j % 2, :], ps[0:rows, bank_of(kind, m), :], ACT.Identity,
                                             scale=mark, bias=add).then_inc(S[kind, "high_ready"], 1)

            def ffn(r):
                def exp_of_logits(c):
                    act.wait_ge(logits_shifted, NC * r + c + 1)
                    t = slice(c * TPC, (c + 1) * TPC)
                    nc.scalar.activation(pr[:, t, :], lg[:, t, :], ACT.Exp).then_inc(exp_logits, 1)

                def turn(c):
                    act.wait_ge(turned, NC * (r + 1) + c + 1)
                    high_part(NC * (2 * r + 2) + c, 6 + c % 2)

                for i in range(UNITS):
                    e, c = divmod(i, NC)
                    for f, (_, rows) in enumerate(FT):
                        j = (UNITS * r + i) * len(FT) + f
                        act.wait_ge(gate_ready, j + 1)
                        if j >= 2:
                            act.wait_ge(hidden_ready, j - 1)
                        nc.scalar.activation(silu[0:rows, j % 2, :], ps[0:rows, j % 2, :], ACT.Silu).then_inc(silu_done, 1)
                    if 1 <= i <= NC:
                        exp_of_logits(i - 1)
                    if r == 0 and e == NEXP - 1 and c >= 2:
                        turn(c - 2)
                if r == 0:
                    turn(2)
                    turn(3)

            act.wait_ge(loaded["cst"], 16)
            for c in range(NC):
                act.wait_ge(turned, c + 1)
                high_part(c, START_BANKS[c])
            attention("A", 1)
            ffn(0)
            act.wait_ge(biases_ready, 1)
            attention("B", 3)
            ffn(1)

        @block.vector
        def _(v):
            n_chain = [0]

            def link(ins):
                ins.then_inc(chain, 1)
                n_chain[0] += 1
                v.wait_ge(chain, n_chain[0])

            def norm_a(i):
                c = i % NC
                for t in range(c * TPC, (c + 1) * TPC):
                    last = nc.vector.bn_stats(stats[:, t, :], x[:, t, :])
                link(last)
                for t in range(c * TPC, (c + 1) * TPC):
                    last = nc.vector.bn_aggr(mv[:, t, :], stats[:, t, :])
                link(last)
                t = slice(c * TPC, (c + 1) * TPC)
                nc.vector.tensor_scalar(ve[:, t], mv[:, t, 1], EPS, None, ALU.add).then_inc(var_ready, 1)

            def norm_b(i):
                c = i % NC
                t = slice(c * TPC, (c + 1) * TPC)
                v.wait_ge(root_ready, i + 1)
                link(nc.vector.tensor_tensor(newton[:], rs[:, t], rs[:, t], ALU.mult))
                link(nc.vector.tensor_tensor(newton[:], newton[:], ve[:, t], ALU.mult))
                link(nc.vector.tensor_scalar(newton[:], newton[:], -0.5, 1.5, ALU.mult, ALU.add))
                link(nc.vector.tensor_tensor(rs[:, t], rs[:, t], newton[:], ALU.mult))
                for q in range(TPC):
                    t = c * TPC + q
                    last = nc.vector.tensor_scalar(xn[:, c % 2, q, :], x[:, t, :], mv[:, t, 0:1], rs[:, t:t + 1],
                                                   ALU.subtract, ALU.mult)
                last.then_inc(norm_ready, 1)

            def low_part(i, bank, signal):
                c = i % NC
                v.wait_ge(high_done, i + 1)
                nc.vector.tensor_tensor(xl[:, c * QC:(c + 1) * QC], ps[:, bank, :],
                                        xh[:, c * QC:(c + 1) * QC].bitcast(F32), ALU.subtract).then_inc(signal, 1)

            def attention(kind, r):
                od = orders[kind]
                full, free = S[kind, "ring_full"], S[kind, "ring_free"]
                for ev in od.events:
                    if ev[0] == "norm_a":
                        n = [m for m, s in enumerate(od.steps) if s == (od.groups - 1, ev[1])][0]
                        v.wait_ge(free, od.at["out", n] + 1)
                        norm_a(NC * r + ev[1])
                    if ev[0] == "norm_b":
                        if ev[1] >= 2:
                            v.wait_ge(full, od.at["turn", ev[1] - 2] + 1)
                        norm_b(NC * r + ev[1])
                    if ev[0] == "weigh":
                        n = ev[1]
                        v.wait_ge(ones_done, (n + 1) * NT // 2)
                        link(nc.vector.reciprocal(rinv[:], ps[:, ONES, :]))
                        v.wait_ge(S[kind, "evacuated"], n + 1)
                        nc.vector.tensor_tensor(ot[:], o_sb[:], rinv[:], ALU.mult).then_inc(weighed, 1)
                    if ev[0] != "ring":
                        continue
                    use = ev[1]
                    m = od.at[use]
                    bank = bank_of(kind, m)
                    v.wait_ge(full, m + 1)
                    if use in od.proj_at:
                        j = od.proj_at[use]
                        v.wait_ge(S[kind, "high_ready"], j + 1)
                        if use[0] == "lat":
                            c = use[1]
                            dst, rows, add = flat[:, c * QC:(c + 1) * QC], P, col("zero")
                        elif use[0] == "k" and od.a:
                            _, g, h, c = use
                            rows, add = KA_ROWS, col("neg_ka", KA_ROWS)
                            dst = kst[0:rows, g % 2, h, c * QC:(c + 1) * QC]
                        elif use[0] == "k":
                            _, g, _, c = use
                            if g and c == 0:
                                v.wait_ge(S[kind, "keys_ready"], 16 * G * g)
                            dst, rows, add = flat[:, c * QC:(c + 1) * QC], P, bias[:, 1, g:g + 1]
                        else:
                            _, n, h = use
                            rows = KA_ROWS if od.a else P
                            add = col("zero", rows) if od.a else bias[:, 0, od.steps[n][0]:od.steps[n][0] + 1]
                            dst = q_slot(od, n, h)[0:rows, :]
                            if n >= Q_STEPS[kind]:
                                v.wait_ge(S[kind, "scores_ready"], od.tile_at[n - Q_STEPS[kind] + 1, 0, 0])
                        nc.vector.scalar_tensor_tensor(dst, ps[0:rows, bank, :], add, tmp[0:rows, j % 2, :].bitcast(F32),
                                                       ALU.add, ALU.subtract).then_inc(free, 1)
                    elif use[0] == "v":
                        _, g, c = use
                        dst = vst[:, g % 2, c * TPC:(c + 1) * TPC, :]
                        if od.a:
                            nc.vector.tensor_copy(dst, ps[:, bank, :].rearrange("p (t d) -> p t d", d=P)).then_inc(free, 1)
                            continue
                        if g >= 2 and c == 0:
                            v.wait_ge(S[kind, "values_done"], od.last_key_of_group[g - 2])
                        width = G * DB
                        for q in range(TPC):
                            ins = nc.vector.tensor_tensor(
                                dst[:, q, :].rearrange("p (h r) -> p h r", r=32)[:, :, 0:DB],
                                ps[:, bank, q * width:(q + 1) * width].rearrange("p (h r) -> p h r", r=DB),
                                bv_sb[:, g * width:(g + 1) * width].rearrange("p (h r) -> p h r", r=DB), ALU.add)
                        ins.then_inc(free, 1)
                    elif use[0] == "max":
                        _, n, h, q, k = use
                        first = od.first_key_chunk(n)
                        lo = P * q if (not od.a and k == first) else 0
                        nc.vector.reduce_max(mx[:, h % 2, q, k:k + 1], ps[:, bank, lo:QC], AX.X).then_inc(free, 1)
                        if q == TPC - 1 and k == NC - 1:
                            v.wait_ge(free, m + 1)
                            link(nc.vector.reduce_max(mq[:, n % 2, h, :], mx[:, h % 2, :, first:NC], AX.X))
                            par, at = (h % 2, CA) if od.a else (n % 2, 32 * h + CB)
                            before = ("shift", n - 2, 0) if not od.a else ("shift", n, h - 2) if h >= 2 else ("shift", n - 1, h + 2)
                            if before[1] >= 0:
                                v.wait_ge(full, od.at[before] + 1)
                            hi = ct[:, par, :, at:at + 1].rearrange("p t a -> p (t a)")
                            lo_part = ct[:, par, :, at + 1:at + 2].rearrange("p t a -> p (t a)")
                            link(nc.vector.tensor_copy(hi, mq[:, n % 2, h, :]))
                            nc.vector.tensor_tensor(lo_part, mq[:, n % 2, h, :], hi.bitcast(F32), ALU.subtract)\
                                .then_inc(S[kind, "shift_parts"], 1)
                    elif use[0] == "shift":
                        _, n, h = use
                        if od.a:
                            nc.vector.tensor_copy(q_slot(od, n, h)[CA:CA + 2, :], ps[CA:CA + 2, bank, :]).then_inc(free, 1)
                        else:
                            dst = q_slot(od, n, 0)
                            nc.vector.tensor_tensor(dst, ps[:, bank, :], dst.bitcast(F32), ALU.add).then_inc(free, 1)
                    elif use[0] == "sums":
                        n = use[1]
                        link(nc.vector.reciprocal(rinv[:], ps[:, bank, :]))
                        nc.vector.tensor_tensor(ot[:], o_sb[:], rinv[:], ALU.mult).then_inc(free, 1)
                    elif use[0] == "turn":
                        low_part(NC * r + use[1], bank, free)
                    elif use[0] == "out":
                        c = od.steps[use[1]][1]
                        xs = x[:, c * TPC:(c + 1) * TPC, :]
                        nc.vector.tensor_tensor(xs, ps[:, bank, :].rearrange("p (t d) -> p t d", d=P), xs, ALU.add)\
                            .then_inc(free, 1)
                v.wait_ge(free, od.uses)
                nc.vector.memset(marker[:, 0:1], 0.0).then_inc(attention_done, 1)
                v.wait_ge(attention_done, 1 if od.a else 2)

            def ffn(r):
                wide = [P, TPC, E]

                def route_a(c):
                    t = slice(c * TPC, (c + 1) * TPC)
                    v.wait_ge(logits_ready, NC * r + c + 1)
                    nc.vector.tensor_copy(lg[:, t, :], ps[:, 6 + c % 2, 0:TPC * E].rearrange("p (t e) -> p t e", e=E))\
                        .then_inc(logits_taken, 1)
                    v.wait_ge(logits_taken, NC * r + c + 1)
                    link(nc.vector.reduce_max(lmax[:, t], lg[:, t, :], AX.X))
                    nc.vector.tensor_tensor(lg[:, t, :], lg[:, t, :], lmax[:, t].rearrange("p (t a) -> p t a", a=1)
                                            .broadcast_to(wide), ALU.subtract).then_inc(logits_shifted, 1)

                def route_b(c):
                    t = slice(c * TPC, (c + 1) * TPC)
                    lsum, lrec = lmax[:, t], lrecip[:, t]

                    def spread(a, n=E):
                        return a.broadcast_to([P, TPC, n])

                    v.wait_ge(exp_logits, NC * r + c + 1)
                    link(nc.vector.reduce_sum(lsum, pr[:, t, :], AX.X))
                    link(nc.vector.reciprocal(lrec, lsum))
                    link(nc.vector.tensor_tensor(pr[:, t, :], pr[:, t, :], spread(lrec.rearrange("p (t a) -> p t a", a=1)),
                                                 ALU.mult))
                    for q in range(c * TPC, (c + 1) * TPC):
                        last = nc.vector.max(top[:, q, :], pr[:, q, :])
                    link(last)
                    for q in range(c * TPC, (c + 1) * TPC):
                        last = nc.vector.max_index(topi[:, q, :], top[:, q, :], pr[:, q, :])
                    link(last)
                    nc.vector.tensor_copy(topf[:, t, :], topi[:, t, 0:2])
                    link(nc.vector.tensor_tensor(lsum, top[:, t, 0], top[:, t, 1], ALU.add))
                    link(nc.vector.reciprocal(lrec, lsum))
                    link(nc.vector.tensor_tensor(wtop[:, t, :], top[:, t, 0:2],
                                                 spread(lrec.rearrange("p (t a) -> p t a", a=1), 2), ALU.mult))
                    iota = cst[:, C_IOTA:C_IOTA + E].rearrange("p (a e) -> p a e", a=1).broadcast_to(wide)
                    for i, dst in enumerate((cw[:, t, :], cw2[:, t, :])):
                        link(nc.vector.tensor_tensor(dst, iota, spread(topf[:, t, i:i + 1]), ALU.is_equal))
                        link(nc.vector.tensor_tensor(dst, dst, spread(wtop[:, t, i:i + 1]), ALU.mult))
                    link(nc.vector.tensor_tensor(cw[:, t, :], cw[:, t, :], cw2[:, t, :], ALU.add))

                def add_down(i):
                    e, c = divmod(i, NC)
                    y = UNITS * r + i
                    v.wait_ge(down_ready, y + 1)
                    if e:
                        v.wait_ge(added, y - NC + 1)
                    for q in range(TPC):
                        t = c * TPC + q
                        src = ps[:, 4 + y % 2, q * P:(q + 1) * P]
                        if e == 0:
                            ins = nc.vector.tensor_tensor(x[:, t, :], src, x[:, t, :], ALU.add)
                        else:
                            ins = nc.vector.scalar_tensor_tensor(x[:, t, :], src, cw[:, t, e - 1:e], x[:, t, :],
                                                                 ALU.mult, ALU.add)
                    ins.then_inc(added, 1)

                def norm_a_after(c):
                    v.wait_ge(added, UNITS * r + (NEXP - 1) * NC + c + 1)
                    norm_a(2 * NC + c)

                def norm_b_after(c):
                    if c >= 2:
                        v.wait_ge(turned, NC + c - 1)
                    norm_b(2 * NC + c)

                for i in range(UNITS):
                    e, c = divmod(i, NC)
                    y = UNITS * r + i
                    for f, (_, rows) in enumerate(FT):
                        j = y * len(FT) + f
                        v.wait_ge(silu_done, j + 1)
                        v.wait_ge(up_ready, j + 1)
                        if f == 0 and y >= 2:
                            v.wait_ge(down_ready, y - 1)
                        nc.vector.tensor_tensor(hid[0:rows, y % 2, f, :], ps[0:rows, 2 + j % 2, :],
                                                silu[0:rows, j % 2, :], ALU.mult).then_inc(hidden_ready, 1)
                        if f == 1 and i:
                            add_down(i - 1)
                    if e == 0:
                        route_a(c)
                    if 1 <= i <= NC:
                        route_b(i - 1)
                    if r == 0 and e == NEXP - 1:
                        if c >= 1:
                            norm_a_after(c - 1)
                            norm_b_after(c - 1)
                        if c >= 2:
                            low_part(2 * NC + c - 2, 6 + c % 2, parts_done)
                add_down(UNITS - 1)
                if r == 0:
                    norm_a_after(NC - 1)
                    low_part(2 * NC + 2, 6, parts_done)
                    norm_b_after(NC - 1)
                    low_part(2 * NC + 3, 7, parts_done)
                v.wait_ge(added, UNITS * (r + 1))

            v.wait_ge(loaded["cst"], 16)
            nc.vector.tensor_copy(identr[:], ident)
            v.wait_ge(loaded["masks"], 16)
            link(nc.vector.tensor_copy(maskr[:], mask_raw))
            for c in range(NC + 2):
                if c < NC:
                    v.wait_ge(loaded["x"][c], 16)
                    norm_a(c)
                    if c >= 2:
                        v.wait_ge(turned, c - 1)
                    norm_b(c)
                if c >= 2:
                    low_part(c - 2, START_BANKS[c - 2], parts_done)
            v.wait_ge(filled, 3)
            attention("A", 1)
            ffn(0)
            v.wait_ge(loaded["b"], 128)
            v.wait_ge(filled, 4)
            link(nc.vector.tensor_scalar(bias[:, 2, :], bias[:, 0, :], col("lo_qb"), None, ALU.mult))
            nc.vector.tensor_scalar(bias[:, 3, :], bias[:, 1, :], col("lo_kb"), None, ALU.mult).then_inc(biases_ready, 1)
            v.wait_ge(biases_ready, 1)
            link(nc.vector.tensor_scalar(bias[:, 1, :], bias[:, 1, :], col("neg_kb"), None, ALU.add))
            link(nc.vector.tensor_tensor(x[:], x[:], bo_sb.rearrange("p (a d) -> p a d", a=1).broadcast_to([P, NT, D]),
                                         ALU.add))
            attention("B", 3)
            ffn(1)

        @block.tensor
        def _(pe):
            mm = nc.tensor.matmul

            def turn(i, bank):
                pe.wait_ge(norm_ready, i + 1)
                c = i % NC
                for q in range(TPC):
                    last = nc.tensor.transpose(ps[:, bank, q * P:(q + 1) * P], xn[:, c % 2, q, :], ident)
                return last

            def three(dst, wh, wl, xs, start=True, stop=True):
                a, b = xs
                mm(dst, wh, a, start=start, stop=False)
                mm(dst, wh, b, start=False, stop=False)
                return mm(dst, wl, a, start=False, stop=stop)

            def attention(kind, r):
                od = orders[kind]
                full, free = S[kind, "ring_full"], S[kind, "ring_free"]
                depth = len(RING[kind])
                for ev in od.events:
                    if ev[0] == "scores":
                        _, n, k, h = ev
                        g, c = od.steps[n]
                        t = od.tile_at[n, k, h]
                        if t >= BANKS:
                            pe.wait_ge(S[kind, "exp_done"], t - BANKS + 1)
                        if k == 0:
                            pe.wait_ge(free, od.at["shift", n, h if od.a else 0] + 1)
                        rows = KA_ROWS if od.a else P
                        rhs = q_slot(od, n, h)[0:rows, :]
                        kt, w, diagonal = od.key_tiles(n)[k]
                        dst = ps[:, t % BANKS, 0:w]
                        last = mm(dst, kst[0:rows, g % 2, h, kt * P:(kt + 1) * P], rhs[:, 0:w],
                                  start=True, stop=not diagonal)
                        if diagonal:
                            last = mm(dst[:, w - P:w], identr[:], maskr[:, 0, :], start=False, stop=True)
                        last.then_inc(S[kind, "scores_ready"], 1)
                    elif ev[0] == "values":
                        _, n, k = ev
                        g, c = od.steps[n]
                        keys = od.key_tiles(n)
                        key = od.key_at[n, k]
                        kt, w, _ = keys[k]
                        pe.wait_ge(S[kind, "exp_done"], G * (key + 1))
                        if k == 0:
                            if n:
                                pe.wait_ge(S[kind, "evacuated"], n)
                            pe.wait_ge(free, od.at["v", g, NC - 1] + 1)
                        for h in range(G):
                            last = mm(ps[32 * h:32 * h + 32, VALUES, 0:w], vst[:, g % 2, kt, 32 * h:32 * h + 32],
                                      prob[:, (G * key + h) % SLOTS, 0:w], start=k == 0, stop=k == len(keys) - 1)
                        last.then_inc(S[kind, "values_done"], 1)
                    elif ev[0] == "ones":
                        pair = ev[1]
                        n, k = divmod(pair, NT // 2)
                        pe.wait_ge(pair_summed, G * (pair + 1))
                        if k == 0 and n:
                            pe.wait_ge(weighed, n)
                        for h in range(G):
                            last = mm(ps[32 * h:32 * h + 32, ONES, :], ones[:], prob[:, (2 * G * pair + h) % SLOTS, :],
                                      start=k == 0, stop=k == NT // 2 - 1)
                        last.then_inc(ones_done, 1)
                    elif ev[0] == "ring":
                        use = ev[1]
                        m = od.at[use]
                        bank = bank_of(kind, m)
                        if m >= depth:
                            pe.wait_ge(free, m - depth + 1)
                        if use[0] == "turn":
                            last = turn(NC * r + use[1], bank)
                        elif use[0] == "lat":
                            c = use[1]
                            wait_parts(pe, 0, c)
                            xs = (xh[:, c * QC:(c + 1) * QC], xl[:, c * QC:(c + 1) * QC])
                            last = three(ps[:, bank, :], wch[:], wcl[:], xs)
                        elif use[0] == "k" and od.a:
                            _, g, h, c = use
                            pe.wait_ge(free, od.at["lat", NC - 1] + 1)
                            dst, rhs = ps[0:KA_ROWS, bank, :], flat[:, c * QC:(c + 1) * QC]
                            mm(dst, wkh[:, g * G + h, :], rhs, start=True, stop=False)
                            last = mm(dst, wkl[:, g * G + h, :], rhs, start=False, stop=True)
                        elif use[0] == "v":
                            _, g, c = use
                            for q in range(TPC) if od.a else []:
                                lhs = flat[:, c * QC + q * P:c * QC + (q + 1) * P]
                                dst = ps[:, bank, q * P:(q + 1) * P]
                                mm(dst, lhs, wvh[:, g * P:(g + 1) * P], start=True, stop=False)
                                last = mm(dst, lhs, wvl[:, g * P:(g + 1) * P], start=False, stop=True)
                            for q in [] if od.a else range(TPC):
                                s = slice(c * QC + q * P, c * QC + (q + 1) * P)
                                w = slice(g * G * DB, (g + 1) * G * DB)
                                dst = ps[:, bank, q * G * DB:(q + 1) * G * DB]
                                mm(dst, xh[:, s], wvbh[:, w], start=True, stop=False)
                                mm(dst, xl[:, s], wvbh[:, w], start=False, stop=False)
                                last = mm(dst, xh[:, s], wvbl[:, w], start=False, stop=True)
                        elif use[0] == "k":
                            _, g, _, c = use
                            xs = (xh[:, c * QC:(c + 1) * QC], xl[:, c * QC:(c + 1) * QC])
                            last = three(ps[:, bank, :], wkbh[:, g, :], wkbl[:, g, :], xs)
                        elif use[0] == "q":
                            _, n, h = use
                            g, c = od.steps[n]
                            xs = (xh[:, c * QC:(c + 1) * QC], xl[:, c * QC:(c + 1) * QC])
                            if od.a:
                                last = three(ps[0:KA_ROWS, bank, :], wqh[:, g * G + h, :], wql[:, g * G + h, :], xs)
                            else:
                                last = three(ps[:, bank, :], wqbh[:, g, :], wqbl[:, g, :], xs)
                        elif use[0] == "max":
                            _, n, h, q, k = use
                            g, c = od.steps[n]
                            if q == 0 and k == od.first_key_chunk(n):
                                pe.wait_ge(free, od.at["q", n, h if od.a else 0] + 1)
                                if od.a:
                                    pe.wait_ge(free, od.at["k", g, G - 1, NC - 1] + 1)
                                else:
                                    pe.wait_ge(S[kind, "keys_ready"], 16 * G * (g + 1))
                            rows = CA if od.a else P
                            diagonal = not od.a and k == c
                            lo = P * q if diagonal else 0
                            lhs = q_slot(od, n, h)[0:rows, q * P:(q + 1) * P]
                            last = mm(ps[:, bank, lo:QC], lhs, kst[0:rows, g % 2, h, k * QC + lo:(k + 1) * QC],
                                      start=True, stop=not diagonal)
                            if diagonal:
                                last = mm(ps[:, bank, lo:lo + P], identr[:], maskr[:, 1, :], start=False, stop=True)
                        elif use[0] == "shift":
                            _, n, h = use
                            if od.a:
                                pe.wait_ge(S[kind, "shift_parts"], G * n + h + 1)
                                rows, par = KA_ROWS, h % 2
                            else:
                                pe.wait_ge(S[kind, "shift_parts"], G * (n + 1))
                                rows, par = P, n % 2
                            for q in range(TPC):
                                last = mm(ps[0:rows, bank, q * P:(q + 1) * P], ct[:, par, q, 0:rows], identr[:],
                                          start=True, stop=True)
                        elif use[0] == "sums":
                            n = use[1]
                            pe.wait_ge(S[kind, "evacuated"], n + 1)
                            last = mm(ps[:, bank, :], sel, o_sb[:], start=True, stop=True)
                        elif use[0] == "out":
                            n = use[1]
                            g, c = od.steps[n]
                            if od.a:
                                pe.wait_ge(weighed, n + 1)
                            else:
                                pe.wait_ge(free, od.at["sums", n] + 1)
                            for q in range(TPC):
                                last = mm(ps[:, bank, q * P:(q + 1) * P], ot[:, q * P:(q + 1) * P],
                                          wo_sb[:, g, :], start=True, stop=True)
                        last.then_inc(full, 1)

            def ffn(r):
                def logits(c):
                    if c >= 2 or r:
                        pe.wait_ge(logits_taken, NC * r + c - 1)
                    for q in range(TPC):
                        s = slice(c * QC + q * P, c * QC + (q + 1) * P)
                        dst = ps[:, 6 + c % 2, q * E:(q + 1) * E]
                        mm(dst, xh[:, s], gwh[:], start=True, stop=False)
                        mm(dst, xl[:, s], gwh[:], start=False, stop=False)
                        mm(dst, xh[:, s], gwl[:], start=False, stop=False)
                        last = mm(dst, xl[:, s], gwl[:], start=False, stop=True)
                    last.then_inc(logits_ready, 1)

                def down(i):
                    n, y = NEXP * r + i // NC, UNITS * r + i
                    pe.wait_ge(hidden_ready, (y + 1) * len(FT))
                    if y >= 2:
                        pe.wait_ge(added, y - 1)
                    for q in range(TPC):
                        for f, (_, rows) in enumerate(FT):
                            last = mm(ps[:, 4 + y % 2, q * P:(q + 1) * P], hid[0:rows, y % 2, f, q * P:(q + 1) * P],
                                      wd[0:rows, n % 2, f, :], start=f == 0, stop=f == len(FT) - 1)
                    last.then_inc(down_ready, 1)

                def turn_after(c):
                    if c >= 2:
                        pe.wait_ge(parts_done, NC + c - 1)
                    turn(2 * NC + c, 6 + c % 2).then_inc(turned, 1)

                kind = "AB"[r]
                pe.wait_ge(S[kind, "exp_done"], orders[kind].tiles)
                pe.wait_ge(S[kind, "ring_free"], orders[kind].uses)
                for i in range(UNITS):
                    e, c = divmod(i, NC)
                    n = NEXP * r + e
                    if c == 0:
                        pe.wait_ge(gu_split, 2 * (n + 1))
                        pe.wait_ge(gu_loaded[n % 2], 48 * (n // 2 + 1))
                    xs = (xh[:, c * QC:(c + 1) * QC], xl[:, c * QC:(c + 1) * QC])
                    for f, (at, rows) in enumerate(FT):
                        j = (UNITS * r + i) * len(FT) + f
                        if j >= 2:
                            pe.wait_ge(silu_done, j - 1)
                        three(ps[0:rows, j % 2, :], wguh[:, n % 2, at:at + rows], wgul[:, n % 2, at:at + rows], xs)\
                            .then_inc(gate_ready, 1)
                        if j >= 2:
                            pe.wait_ge(hidden_ready, j - 1)
                        three(ps[0:rows, 2 + j % 2, :], wguh[:, n % 2, I + at:I + at + rows],
                              wgul[:, n % 2, I + at:I + at + rows], xs).then_inc(up_ready, 1)
                        if f == 0 and i:
                            down(i - 1)
                    if e == 0:
                        logits(c)
                    if r == 0 and e == NEXP - 1 and c >= 2:
                        turn_after(c - 2)
                if r == 0:
                    turn_after(2)
                down(UNITS - 1)
                if r == 0:
                    turn_after(3)

            pe.wait_ge(loaded["cst"], 16)
            for c in range(NC):
                turn(c, START_BANKS[c]).then_inc(turned, 1)
            pe.wait_ge(filled, 3)
            pe.wait_ge(weights_split, split_count("gw"))
            attention("A", 1)
            ffn(0)
            for c in range(NC):
                wait_parts(pe, 2, c)
            pe.wait_ge(weights_split, split_count("wvb"))
            pe.wait_ge(filled, 6)
            pe.wait_ge(added, UNITS)
            attention("B", 3)
            ffn(1)


def stack_heads(w, heads, width, parts, pitch):
    w = w.reshape(w.shape[0], heads, width)
    zero = np.zeros((w.shape[0], heads, pitch - parts * width), w.dtype)
    return np.concatenate([w] * parts + [zero], axis=2)


def kernel(L0_attn_a_x, L0_attn_a_Wq, L0_attn_a_Wkv_down, L0_attn_a_Wk_up, L0_attn_a_Wv_up, L0_attn_a_Wo,
           L0_attn_b_w_qkv, L0_attn_b_b_qkv, L0_attn_b_w_out, L0_attn_b_b_out, L0_ffn_gate_w,
           L0_ffn_base_wgu, L0_ffn_base_wd, L0_ffn_exp_wgu, L0_ffn_exp_wd):
    import concourse.bacc as bacc
    from concourse.bass_utils import run_bass_kernel_spmd

    f = lambda a: np.asarray(a)
    x = f(L0_attn_a_x).reshape(T, D)
    wqkv, bqkv = f(L0_attn_b_w_qkv), f(L0_attn_b_b_qkv)
    b3 = bqkv.reshape(3, 1, D)
    bias_cols = lambda b: stack_heads(b, HB, DB, 3, 32).reshape(GB, P).T
    wob = f(L0_attn_b_w_out).reshape(HB, DB, D)
    wob = np.concatenate([wob, np.zeros((HB, 32 - DB, D), wob.dtype)], axis=1)
    wk = f(L0_attn_a_Wk_up).T
    wv = f(L0_attn_a_Wv_up).T
    kv = f(L0_attn_a_Wkv_down).T
    arrays = {
        "x": x,
        "wq_a": stack_heads(f(L0_attn_a_Wq).T, HA, DA, 3, KA_ROWS),
        "wkv_a": np.concatenate([kv, kv], axis=1),
        "wk_a": stack_heads(np.concatenate([wk, wk], axis=0), HA, DA, 3, KA_ROWS),
        "wv_a": np.concatenate([wv, wv], axis=0),
        "wo_a": f(L0_attn_a_Wo).T.reshape(GA, P, D).transpose(1, 0, 2),
        "wq_b": stack_heads(wqkv[:, 0:D], HB, DB, 3, 32).reshape(D, GB, P),
        "wk_b": stack_heads(wqkv[:, D:2 * D], HB, DB, 3, 32).reshape(D, GB, P),
        "wv_b": wqkv[:, 2 * D:3 * D],
        "bq_b": bias_cols(b3[0]),
        "bk_b": bias_cols(b3[1]),
        "bv_b": b3[2],
        "wo_b": wob.reshape(GB, P, D).transpose(1, 0, 2),
        "bo_b": f(L0_attn_b_b_out).reshape(1, D),
        "gate_w": f(L0_ffn_gate_w),
        "base_wgu": f(L0_ffn_base_wgu),
        "base_wd": f(L0_ffn_base_wd),
        "exp_wgu": f(L0_ffn_exp_wgu),
        "exp_wd": f(L0_ffn_exp_wd),
        "consts": constants(),
        "masks": diagonal_masks(),
    }
    arrays = {n: np.ascontiguousarray(a) for n, a in arrays.items()}
    nc = bacc.Bacc("TRN2", target_bir_lowering=False, num_devices=1)
    args = [nc.dram_tensor("in_" + n, a.shape, mybir.dt.from_np(a.dtype), kind="ExternalInput").ap()
            for n, a in arrays.items()]
    out = nc.dram_tensor("out_x", (T, D), F32, kind="ExternalOutput").ap()
    build(nc, *args, out)
    r = run_bass_kernel_spmd(nc, [{"in_" + n: a for n, a in arrays.items()}], core_ids=[0])
    return r.results[0]["out_x"].reshape(1, T, D)
```

```python
import numpy as np
import concourse.bass as bass
from concourse import mybir
from contextlib import ExitStack

F32 = mybir.dt.float32
F32R = mybir.dt.float32r
U32 = mybir.dt.uint32
ALU = mybir.AluOpType
ACT = mybir.ActivationFunctionType
AX = mybir.AxisListType

P = 128
T, D = 2048, 128
NT = T // P
QC = 512
NC = T // QC
TPC = QC // P
G = 4
HA, DA, RANK = 8, 32, 64
HB, DB = 16, 8
GA, GB = HA // G, HB // G
E, I = 8, 352
FT = [(0, 128), (128, 128), (256, 96)]
EPS = 1e-5
MASKED = -1e38
SA = 32
CA = 3 * SA
KA_ROWS = CA + 2
CB = 3 * DB
BANKS = 3
RING = {"A": [3, 4, 5], "B": [3, 4, 5, 7]}
VALUES, ONES = 6, 7
START_TURN_BANK = 7
TAIL_OUT, TAIL_TURN = 7, 5
START_BANKS = [0, 1, 2, 7]
SLOTS = 18

C_ID, C_COL = 0, 128
COLS = ["lo_qa", "lo_ka", "lo_lat", "neg_ka", "lo_qb", "lo_kb", "neg_kb", "zero"]
C_IOTA = C_COL + len(COLS)
C_ALL = C_IOTA + E


def constants():
    c = np.zeros((P, C_ALL), np.float32)
    r = np.arange(P)
    c[:, C_ID:C_ID + P] = np.eye(P)
    cols = {
        "lo_qa": (r // SA == 1),
        "lo_ka": (r // SA == 2),
        "lo_lat": (r >= RANK),
        "neg_ka": -1.0 * ((r == CA) | (r == CA + 1)),
        "lo_qb": (r % 32 // DB == 1),
        "lo_kb": (r % 32 // DB == 2),
        "neg_kb": -1.0 * ((r % 32 == CB) | (r % 32 == CB + 1)),
        "zero": 0 * r,
    }
    for i, n in enumerate(COLS):
        c[:, C_COL + i] = cols[n]
    c[:, C_IOTA:C_IOTA + E] = np.arange(E)[None, :]
    return c


def diagonal_masks():
    r = np.arange(P)
    return np.stack([np.where(r[None, :] > r[:, None], MASKED, 0),
                     np.where(r[None, :] < r[:, None], MASKED, 0)], axis=1).astype(np.float32)


class Order:

    BEHIND = 2
    LAG = 0.25

    def __init__(self, kind):
        self.kind = kind
        self.a = kind == "A"
        self.groups = GA if self.a else GB
        if self.a:
            self.steps = [(g, c) for g in range(GA) for c in range(NC)]
        else:
            self.steps = [(g, c) for g in range(GB) for c in (range(NC) if g % 2 else reversed(range(NC)))]
        self.ahead = 1 if self.a else 3
        self.events = []
        self.at, self.uses, self.use_at = {}, 0, []
        self.freed_at, self.freed_by = {}, {"vector": 0, "activation": 0}
        self.proj_at, self.projections = {}, 0
        self.tile_at, self.tiles = {}, 0
        self.key_at, self.key_count = {}, 0
        self.last_tile_of_group, self.last_key_of_group = {}, {}
        self.tensor, self.vector, self.activation = 0.0, 0.0, 0.0
        self.freed, self.ready, self.exp_done = [], {}, []
        self.build()

    def key_tiles(self, n):
        g, c = self.steps[n]
        if self.a:
            return [(k, QC, False) for k in range(NT)]
        ks = [(c * TPC + d, (d + 1) * P, True) for d in reversed(range(TPC))]
        return ks + [(k, QC, False) for k in range((c + 1) * TPC, NT)]

    def first_key_chunk(self, n):
        return 0 if self.a else self.steps[n][1]

    def width(self, n, q, k):
        return QC - P * q if not self.a and k == self.first_key_chunk(n) else QC

    def adder(self, n, k, h):
        if not self.a or k % 2 == 0:
            return None
        return "vector" if n == len(self.steps) - 1 and h >= G // 2 else "pool"

    def costs(self, use):
        kind = use[0]
        if kind == "max":
            w = self.width(use[1], *use[3:])
            return 0.0004 * w + (0.06 if w < QC or not self.a else 0), 0.06 + w / 960
        return {"q": (0.65, 0.7), "k": (0.45 if self.a else 0.65, 0.7), "lat": (0.65, 0.7), "v": (0.4, 0.6),
                "shift": (0.3, 0.65), "out": (0.9, 0.65), "turn": (0.3, 0.65)}[kind]

    def freer(self, use):
        return "activation" if self.a and use[0] in ("v", "shift") else "vector"

    def ring(self, *use):
        bank_free = self.freed[self.uses - len(RING[self.kind])] if self.uses >= len(RING[self.kind]) else 0
        pe, dve = self.costs(use)
        self.tensor = max(self.tensor, bank_free, self.when(use)) + pe
        who, done = self.freer(use), self.tensor
        if who == "activation" or use[0] in ("q", "k", "lat", "turn"):
            self.activation = done = max(self.activation, done + self.LAG) + 0.5
        if who == "vector":
            self.vector = done = max(self.vector, done + self.LAG) + dve
        self.freed.append(done + self.LAG)
        self.ready[use] = done + self.LAG
        self.use_at.append(use)
        self.freed_at[use] = self.freed_by[who]
        self.freed_by[who] += 1
        if use[0] == "max" and use[3] == TPC - 1 and use[4] == NC - 1 and (self.a or use[2] == G - 1):
            self.vector += 0.4
            self.ready["parts", use[1], use[2]] = self.vector + 3 * self.LAG
        self.at[use] = self.uses
        self.uses += 1
        if use[0] in ("q", "k", "lat"):
            self.proj_at[use] = self.projections
            self.projections += 1
        self.events.append(("ring", use))

    def for_group(self, g):
        heads = range(G) if self.a else [0]
        return [("k", g, h, c) for c in range(NC) for h in heads] + [("v", g, c) for c in range(NC)]

    def for_queries(self, n):
        kcs = range(self.first_key_chunk(n), NC)
        out = [("q", n, h) for h in (range(G) if self.a else [0])]
        for h in range(G):
            out += [("max", n, h, q, k) for q in range(TPC) for k in kcs]
            if self.a or h == G - 1:
                out.append(("shift", n, h if self.a else 0))
        return out

    def when(self, use):
        if use[0] == "max":
            _, n, h, _, _ = use
            keys = self.ready.get(("k", self.steps[n][0], G - 1 if self.a else 0, NC - 1), 0)
            return max(self.ready[("q", n, h if self.a else 0)], keys + (0 if self.a else 4))
        if use[0] == "shift":
            return self.ready["parts", use[1], use[2] if self.a else G - 1]
        return 0

    def prepare(self, todo):
        depth = len(RING[self.kind])
        while True:
            start = max(self.tensor, self.exp_done[self.tiles - BANKS] if self.tiles >= BANKS else 0)
            if self.uses >= depth and self.freed[self.uses - depth] > start:
                return
            use = self.next_of(todo)
            if use is None:
                return
            self.ring(*use)

    def scores(self, n, k, h):
        _, width, diagonal = self.key_tiles(n)[k]
        self.events.append(("scores", n, k, h))
        start = max(self.tensor, self.exp_done[self.tiles - BANKS] if self.tiles >= BANKS else 0)
        self.tensor = start + 0.22 * width / QC + (0.06 if diagonal else 0)
        self.activation = max(self.activation, self.tensor + self.LAG) + 0.06 + width / 1200
        self.exp_done.append(self.activation + self.LAG)
        self.tile_at[n, k, h] = self.tiles
        self.tiles += 1

    def next_of(self, todo, force=False):
        if not todo:
            return None
        if force or self.when(todo[0]) <= self.tensor:
            return todo.pop(0)
        if todo[0][0] == "shift" and len(todo) > 1:
            use = todo[1]
            if (use[0] == "q" or use[0] == "max" and use[3] < TPC - 1) and self.when(use) <= self.tensor:
                return todo.pop(1)
        return None

    def build(self):
        if self.a:
            for c in range(NC):
                self.ring("lat", c)
        first = self.for_group(0)
        if not self.a:
            early = [("k", 0, 0, 0), ("k", 0, 0, 1), ("v", 0, 0), ("v", 0, 1)]
            for use in early:
                self.ring(*use)
                first.remove(use)
            self.events.append(("last_turn",))
        for use in first + self.for_queries(0):
            self.ring(*use)
        last = len(self.steps) - 1
        planned = 0
        todo, late = [], []
        for n, (g, c) in enumerate(self.steps):
            keys = self.key_tiles(n)
            if n % NC == 0 and g + 1 < self.groups:
                todo = self.for_group(g + 1) + todo
            while planned < min(last, n + self.ahead):
                planned += 1
                todo += self.for_queries(planned)
            for u in range(G * len(keys)):
                k, h = divmod(u, G)
                self.scores(n, k, h)
                if n == last and u == G:
                    self.events.append(("first_expert", n))
                if h == 0:
                    self.key_at[n, k] = self.key_count
                    self.key_count += 1
                for item in [x for x in late if x[0] <= u]:
                    late.remove(item)
                    self.do(item[1], late, u)
                self.prepare(todo)
                self.products(n, k, h, late, u)
                self.prepare(todo)
            while todo and any(x[0] in ("q", "max", "shift") and x[1] == n + 1 for x in todo):
                self.ring(*(self.next_of(todo) or self.next_of(todo, force=True)))
            late = [(max(0, at - G * len(keys)), ev) for at, ev in late]
            self.last_tile_of_group[g] = self.tiles
            self.last_key_of_group[g] = self.key_count
        keys = len(self.key_tiles(last))
        self.values((last, keys - 1), late, 0)
        if self.a:
            self.ones(self.key_count // 2 - 2)
            self.ones(self.key_count // 2 - 1)
            late.append((0, ("weigh", last)))
        while late[0][1] != ("out", last):
            self.do(late.pop(0)[1], late, 0)
        self.freed_before_tail = dict(self.freed_by)
        main, self.events = self.events, []
        while late:
            self.do(late.pop(0)[1], late, 0)
        self.events, self.tail = main, [[ev] for ev in self.events]

    def do(self, ev, late, u):
        if ev[0] in ("out", "turn"):
            self.ring(*ev)
        else:
            self.events.append(ev)
            self.vector += {"weigh": 1.6, "norm_a": 1.5, "norm_b": 1.5}.get(ev[0], 0)
        n = ev[1]
        follow = {"weigh": (2 if self.a else 3, ("scale", n)), "scale": (3 if self.a else 4, ("out", n))}.get(ev[0])
        if ev[0] == "out" and self.steps[n][0] == self.groups - 1:
            follow = (2, ("norm_a", self.steps[n][1]))
        if ev[0] == "norm_a":
            follow = (3, ("norm_b", n))
        if ev[0] == "norm_b":
            follow = (4, ("turn", n))
        if follow:
            late.append((u + follow[0], follow[1]))

    def products(self, n, k, h, late, u):
        at = (n, k - 1) if k else (n - 1, len(self.key_tiles(n - 1)) - 1)
        if h == self.BEHIND and at[0] >= 0:
            self.values(at, late, u)
        count = self.key_count - 1
        if self.a and h == 0 and count % 2 == 0 and count >= 4:
            pair = (count - 4) // 2
            self.ones(pair)
            if pair % (NT // 2) == NT // 2 - 1:
                late.append((u + 1, ("weigh", pair // (NT // 2))))

    def values(self, at, late, u):
        self.events.append(("values", *at))
        width = self.key_tiles(at[0])[at[1]][1]
        exp_done = self.exp_done[G * self.key_at[at] + G - 1]
        self.tensor = max(self.tensor, exp_done) + max(0.15, width / QC)
        if at[1] == len(self.key_tiles(at[0])) - 1:
            self.events.append(("evacuate", at[0]))
            if not self.a:
                late.append((u + 3, ("weigh", at[0])))

    def ones(self, pair):
        self.events.append(("ones", pair))
        self.tensor += 1.0


def build(nc, x_in, wq_a, wkv_a, wk_a, wv_a, wo_a, wq_b, wk_b, wv_b, bq_b, bk_b, bv_b, wo_b, bo_b,
          gate_w, base_wgu, base_wd, exp_wgu, exp_wd, consts, masks, out):
    orders = {"A": Order("A"), "B": Order("B")}
    ctx = ExitStack()
    with ctx:
        def sb(name, shape, dt=F32):
            return ctx.enter_context(nc.sbuf_tensor(name, shape, dt))

        def sem(name):
            return ctx.enter_context(nc.semaphore(name))

        cst = sb("cst", [P, C_ALL])
        ident = cst[:, C_ID:C_ID + P]
        identr = sb("identr", [P, P], F32R)
        maskr = sb("maskr", [P, 2, P], F32R)
        ones = sb("ones", [P, 32])
        x = sb("x", [P, NT, D])
        xh = sb("xh", [P, T], F32R)
        xl = sb("xl", [P, T], F32R)
        kst = sb("kst", [P, 2, G, T], F32R)
        qst = sb("qst", [P, 2, G, QC], F32R)
        vst = sb("vst", [P, 2, NT, P])
        prob = sb("prob", [P, SLOTS, QC])
        tmp = sb("tmp", [P, 2, QC], F32R)
        flat = sb("flat", [P, T], F32R)
        mx = sb("mx", [P, G, TPC, NC])
        mq = sb("mq", [P, 2, G, TPC])
        ct = sb("ct", [P, 2, TPC, P], F32R)
        o_sb = sb("o_sb", [P, QC])
        rinv = sb("rinv", [P, QC])
        rc = sb("rc", [P, QC // 32])
        ot = sb("ot", [P, QC])
        spare = prob[:].rearrange("p a n -> p (a n)")

        def in_spare(at, *shape):
            n = int(np.prod(shape))
            names = "abc"[:len(shape)]
            a = spare[:, at:at + n]
            if len(shape) == 1:
                return a
            return a.rearrange(f"p ({' '.join(names)}) -> p {' '.join(names)}", **dict(zip(names, shape)))

        xn = sb("xn", [P, 2, TPC, D])

        stats = sb("stats", [P, NT, 6])
        mv = sb("mv", [P, NT, 2])
        marker = sb("marker", [P, 2])
        ve = sb("ve", [P, NT])
        rs = sb("rs", [P, NT])
        newton = sb("newton", [P, TPC])
        minus_half = sb("minus_half", [P, TPC])
        mask_raw = in_spare(3072, 2, P)
        wq_raw, wqh, wql = in_spare(0, HA, KA_ROWS), sb("wqh", [P, HA, KA_ROWS], F32R), sb("wql", [P, HA, KA_ROWS], F32R)
        wk_raw, wkh, wkl = in_spare(1024, HA, KA_ROWS), sb("wkh", [P, HA, KA_ROWS], F32R), sb("wkl", [P, HA, KA_ROWS], F32R)
        wv_raw, wvh, wvl = in_spare(2048, HA * DA), sb("wvh", [P, HA * DA], F32R), sb("wvl", [P, HA * DA], F32R)
        wc_raw, wch, wcl = in_spare(2048 + HA * DA, P), sb("wch", [P, P], F32R), sb("wcl", [P, P], F32R)
        wqb_raw, wkb_raw, wvb_raw = (a.rearrange("p (g n) -> p g n", n=P) for a in (o_sb[:], rinv[:], ot[:]))
        wvb_raw = wvb_raw[:, 0, :]
        wqbh, wqbl, wkbh, wkbl = (w[:].rearrange("p h n -> p (h n)")[:, 0:GB * P].rearrange("p (g n) -> p g n", n=P)
                                  for w in (wqh, wql, wkh, wkl))
        wvbh, wvbl = wch[:], wcl[:]
        wo_sb = sb("wo_sb", [P, GB, D])
        bias = sb("bias", [P, 4, GB])
        bv_sb = sb("bv_sb", [P, D])
        bo_sb = ot[:, P:P + D]
        gw_raw, gwh, gwl = sb("gw_raw", [P, E]), sb("gwh", [P, E], F32R), sb("gwl", [P, E], F32R)
        wgu = vst[:, 0, :, :].rearrange("p t d -> p (t d)")[:, 0:4 * I].rearrange("p (a n) -> p a n", a=2)
        wd = [tmp[:, par, 0:len(FT) * D].bitcast(F32).rearrange("p (f d) -> p f d", d=D) for par in range(2)]
        split_at = [qst[:, par, :, :].rearrange("p h n -> p (h n)") for par in range(2)]
        wguh, wgul = ([a[:, i * 2 * I:(i + 1) * 2 * I] for a in split_at] for i in range(2))
        silu = in_spare(0, 2, QC)
        hid = in_spare(2 * QC, 2, len(FT), QC)
        lg, pr, top, cw2 = (in_spare(8 * QC + i * P, NT, E) for i in range(4))
        lmax = sb("lmax", [P, NT])
        lrecip = sb("lrecip", [P, NT])
        topi = in_spare(16 * QC + P, NT, 8).bitcast(U32)
        topf = sb("topf", [P, NT, 2])
        wtop = sb("wtop", [P, NT, 2])
        cw = sb("cw", [P, NT, E])

        ps = ctx.enter_context(nc.psum_tensor("ps", [P, 8, QC], F32))

        def bank_of(kind, m):
            od = orders[kind]
            for part, bank in ((0, TAIL_OUT), (3, TAIL_TURN)):
                if od.at[od.tail[part][0][1]] == m:
                    return bank
            return RING[kind][m % len(RING[kind])]

        def q_slot(od, n, h):
            return qst[:, n % 2, h if od.a else n // 2 % G, :]

        Q_STEPS = {"A": 2, "B": 2 * G}

        def col(name, rows=P):
            i = C_COL + COLS.index(name)
            return cst[0:rows, i:i + 1]

        loaded = {n: sem("loaded_" + n) for n in ("cst", "qa", "ca", "ka", "va", "small", "b", "masks")}
        loaded["x"] = [sem(f"loaded_x{c}") for c in range(NC)]
        weights_split = sem("weights_split")
        filled = sem("filled")
        S = {}
        for kind in "AB":
            for n in ("scores_ready", "exp_done", "values_done", "ring_full", "freed_by_vector", "freed_by_activation",
                      "high_ready", "evacuated", "inverted", "weighed", "shift_parts", "keys_ready"):
                S[kind, n] = sem(n + "_" + kind)
        chain = sem("vector_chain")
        pair_summed = {who: sem("pair_summed_by_" + who) for who in ("pool", "vector")}
        ones_done = sem("ones_done")
        var_ready, root_ready = sem("var_ready"), sem("root_ready")
        norm_ready, turned, high_done, parts_done = sem("norm_ready"), sem("turned"), sem("high_done"), sem("parts_done")
        logits_taken = sem("logits_taken")
        logits_ready, logits_shifted, exp_logits = sem("logits_ready"), sem("logits_shifted"), sem("exp_logits")
        gu_loaded = [sem("gu_loaded0"), sem("gu_loaded1")]
        gu_split, gate_ready, up_ready, silu_done, hidden_ready, down_ready, added = (
            sem(n) for n in ("gu_split", "gate_ready", "up_ready", "silu_done", "hidden_ready", "down_ready", "added"))
        stored = sem("stored")
        attention_done, biases_ready, bias_added = sem("attention_done"), sem("biases_ready"), sem("bias_added")

        NEXP = E + 1
        UNITS = NEXP * NC
        JOBS = NC * len(FT)

        LOOP_FIRST, LOOP_TIMES = 2, (NEXP - 3) // 2

        def plus(count, more, per_expert):
            return count if isinstance(more, int) else more * per_expert + count

        def walk_units(queue, unit):
            def expert(e, more=0):
                for c in range(NC):
                    unit(e, c, more)

            expert(0)
            expert(1)
            with queue.Fori(0, LOOP_TIMES) as times:
                for e in (LOOP_FIRST, LOOP_FIRST + 1):
                    expert(e, times * 2)
            expert(NEXP - 1)

        def loads_of(r, e):
            return r * (NEXP + 1 - e % 2) // 2 + e // 2 + 1

        SPLITS = ["wc", "wk", "wq", "wv", "gw", "wqb", "wkb", "wvb"]

        def split_count(name):
            return 2 * (SPLITS.index(name) + 1)

        def wait_freed(eng, kind, *use):
            od = orders[kind]
            eng.wait_ge(S[kind, "freed_by_" + od.freer(use)], od.freed_at[use] + 1)

        def wait_all_freed(eng, kind):
            for who, count in orders[kind].freed_before_tail.items():
                if count:
                    eng.wait_ge(S[kind, "freed_by_" + who], count)

        def tail_after(i, f):
            return {(0, 1): 0, (0, 2): 1, (1, 0): 2, (1, 1): 3}.get((i, f))

        def wait_parts(eng, r, c):
            if r % 2 == 0:
                eng.wait_ge(parts_done, NC * (r // 2) + c + 1)
            else:
                kind = "AB"[r // 2]
                wait_freed(eng, kind, "turn", c)

        def add_pair(queue, engine, od, n, k, h):
            key = od.key_at[n, k]
            queue.wait_ge(S["A", "exp_done"], G * key + h + 1)
            queue.wait_ge(S["A", "values_done"], key)
            first, second = prob[:, (G * (key - 1) + h) % SLOTS, :], prob[:, (G * key + h) % SLOTS, :]
            engine.tensor_tensor(first, first, second, ALU.add).then_inc(pair_summed[od.adder(n, k, h)], 1)

        def split_expert(queue, engine, r, e):
            par, n = e % 2, NEXP * r + e
            queue.wait_ge(gu_loaded[par], 48 * loads_of(r, e))
            if n:
                queue.wait_ge(gu_split, 2 * n)
            if e >= 2:
                queue.wait_ge(up_ready, len(FT) * NC * (n - 1))
            else:
                od = orders["AB"[r]]
                tiles = od.tile_at[len(od.steps) - 1, 0, 0] if e == 0 else od.tiles
                queue.wait_ge(S["AB"[r], "scores_ready"], tiles)
            engine.tensor_copy(wguh[par], wgu[:, par, :]).then_inc(gu_split, 1)
            queue.wait_ge(gu_split, 2 * n + 1)
            engine.tensor_tensor(wgul[par], wgu[:, par, :], wguh[par].bitcast(F32), ALU.subtract)\
                .then_inc(gu_split, 1)

        block = ctx.enter_context(nc.Block())

        @block.sync
        def _(sp):
            for c in range(NC):
                sp.dma_start(x[:, c * TPC:(c + 1) * TPC, :],
                             x_in[c * QC:(c + 1) * QC, :].rearrange("(t p) d -> p t d", p=P)).then_inc(loaded["x"][c], 16)
                if c == 0:
                    sp.dma_start(cst[:], consts).then_inc(loaded["cst"], 16)
            sp.dma_start(wc_raw, wkv_a).then_inc(loaded["ca"], 16)
            sp.dma_start(wk_raw, wk_a).then_inc(loaded["ka"], 16)
            sp.dma_start(wq_raw, wq_a).then_inc(loaded["qa"], 16)
            sp.dma_start(wv_raw, wv_a).then_inc(loaded["va"], 16)
            sp.dma_start(wo_sb[:, 0:GA, :], wo_a).then_inc(loaded["small"], 16)
            sp.dma_start(gw_raw[:], gate_w).then_inc(loaded["small"], 16)
            sp.dma_start(mask_raw, masks).then_inc(loaded["masks"], 16)
            def load_b():
                for dst, src in ((wqb_raw, wq_b), (wkb_raw, wk_b), (wvb_raw, wv_b), (wo_sb[:], wo_b),
                                 (bias[:, 0, :], bq_b), (bias[:, 1, :], bk_b)):
                    sp.dma_start(dst, src).then_inc(loaded["b"], 16)
                sp.dma_start(bv_sb[:], bv_b.broadcast_to([P, D])).then_inc(loaded["b"], 16)
                sp.dma_start(bo_sb, bo_b.broadcast_to([P, D])).then_inc(loaded["b"], 16)

            def load_expert(r, e, gu, down):
                par, n = e % 2, NEXP * r + e
                if e >= 2:
                    sp.wait_ge(gu_split, 2 * (n - 1))
                    sp.wait_ge(down_ready, NC * (n - 1))
                elif e == 0:
                    od = orders["AB"[r]]
                    last_use = max(od.proj_at, key=od.proj_at.get)
                    wait_freed(sp, "AB"[r], *last_use)
                    sp.wait_ge(S["AB"[r], "values_done"], od.last_key_of_group[od.groups - 2])
                sp.dma_start(wgu[:, par, :], gu).then_inc(gu_loaded[par], 16)
                sp.dma_start(wd[par][:, 0:2, :], down[0:256, :].rearrange("(f p) d -> p f d", p=P)).then_inc(gu_loaded[par], 16)
                sp.dma_start(wd[par][0:96, 2, :], down[256:I, :]).then_inc(gu_loaded[par], 16)

            def load_experts(r):
                load_expert(r, 0, base_wgu, base_wd)
                load_expert(r, 1, exp_wgu[0], exp_wd[0])
                if r == 0:
                    sp.wait_ge(attention_done, 1)
                    load_b()
                for e in range(1, E):
                    load_expert(r, e + 1, exp_wgu[e], exp_wd[e])

            load_experts(0)
            od = orders["B"]
            for g in range(GB):
                wait_freed(sp, "B", "k", g, 0, NC - 1)
                if g == 0:
                    sp.wait_ge(filled, 6)
                if g >= 2:
                    sp.wait_ge(S["B", "scores_ready"], od.last_tile_of_group[g - 2])
                for h in range(G):
                    sp.dma_start(kst[32 * h:32 * h + 32, g % 2, h, :].bitcast(F32),
                                 flat[32 * h:32 * h + 32, :].bitcast(F32)).then_inc(S["B", "keys_ready"], 16)
            load_experts(1)
            for c in range(NC):
                sp.wait_ge(added, NEXP * NC + (NEXP - 1) * NC + c + 1)
                sp.dma_start(out[c * QC:(c + 1) * QC, :].rearrange("(t p) d -> p t d", p=P),
                             x[:, c * TPC:(c + 1) * TPC, :]).then_inc(stored, 16)
            sp.wait_ge(stored, 16 * NC)

        @block.gpsimd
        def _(pool):
            n_split = [0]

            def split(hi, lo, raw):
                nc.gpsimd.tensor_copy(hi, raw).then_inc(weights_split, 1)
                n_split[0] += 1
                pool.wait_ge(weights_split, n_split[0])
                nc.gpsimd.tensor_tensor(lo, raw, hi.bitcast(F32), ALU.subtract).then_inc(weights_split, 1)
                n_split[0] += 1

            def power(i):
                c = i % NC
                pool.wait_ge(var_ready, i + 1)
                t = slice(c * TPC, (c + 1) * TPC)
                nc.gpsimd.tensor_tensor(rs[:, t], ve[:, t], minus_half[:], ALU.pow).then_inc(root_ready, 1)

            def attention(kind, r, events=None):
                od = orders[kind]
                for ev in events or od.events:
                    if ev[0] == "norm_a":
                        power(NC * r + ev[1])
                    elif ev[0] == "scale" and ev[1] < len(od.steps) - 1:
                        n = ev[1]
                        pool.wait_ge(S[kind, "evacuated"], n + 1)
                        pool.wait_ge(S[kind, "inverted"], n + 1)
                        if n:
                            wait_freed(pool, kind, "out", n - 1)
                        nc.gpsimd.tensor_tensor(ot[:], o_sb[:], rinv[:], ALU.mult).then_inc(S[kind, "weighed"], 1)
                    elif ev[0] == "scores" and od.adder(*ev[1:]) == "pool":
                        add_pair(pool, nc.gpsimd, od, *ev[1:])

            nc.gpsimd.memset(minus_half[:], -0.5).then_inc(filled, 1)
            nc.gpsimd.memset(ones[:], 1.0).then_inc(filled, 1)
            nc.gpsimd.memset(ct[:].bitcast(F32), 0.0).then_inc(filled, 1)
            pool.wait_ge(filled, 1)
            for c in range(NC):
                power(c)
            pool.wait_ge(loaded["ca"], 16)
            split(wch[:], wcl[:], wc_raw)
            pool.wait_ge(loaded["ka"], 16)
            split(wkh[:], wkl[:], wk_raw)
            pool.wait_ge(loaded["qa"], 16)
            split(wqh[:], wql[:], wq_raw)
            pool.wait_ge(loaded["va"], 16)
            split(wvh[:], wvl[:], wv_raw)
            pool.wait_ge(loaded["small"], 32)
            split(gwh[:], gwl[:], gw_raw[:])

            attention("A", 1)
            attention("A", 1, orders["A"].tail[1])
            split_expert(pool, nc.gpsimd, 0, 1)
            pool.wait_ge(attention_done, 1)
            nc.gpsimd.memset(ct[:].bitcast(F32), 0.0).then_inc(filled, 1)
            nc.gpsimd.memset(vst[:, 1, :, :], 1.0).then_inc(filled, 1)
            nc.gpsimd.memset(kst[:].bitcast(F32), 0.0).then_inc(filled, 1)
            pool.wait_ge(loaded["b"], 128)
            split(wqbh[:], wqbl[:], wqb_raw)
            split(wkbh[:], wkbl[:], wkb_raw)
            split(wvbh[:], wvbl[:], wvb_raw)
            for e in range(2, NEXP):
                split_expert(pool, nc.gpsimd, 0, e)
            pool.wait_ge(gu_split, 2 * NEXP)
            nc.gpsimd.memset(vst[:, 0, :, :], 1.0).then_inc(filled, 1)
            for c in range(NC):
                power(2 * NC + c)
            pool.wait_ge(norm_ready, 3 * NC)
            nc.gpsimd.tensor_tensor(x[:], x[:], bo_sb.rearrange("p (a d) -> p a d", a=1).broadcast_to([P, NT, D]),
                                    ALU.add).then_inc(bias_added, 1)
            pool.wait_ge(bias_added, 1)
            attention("B", 3)
            attention("B", 3, orders["B"].tail[1])
            for e in range(1, NEXP):
                split_expert(pool, nc.gpsimd, 1, e)

        @block.scalar
        def _(act):
            def high_part(i, bank):
                c = i % NC
                nc.scalar.activation(xh[:, c * QC:(c + 1) * QC], ps[:, bank, :], ACT.Identity).then_inc(high_done, 1)

            def attention(kind, r, events=None):
                od = orders[kind]
                bias_cols = {"q": lambda g: bias[:, 2, g:g + 1], "k": lambda g: bias[:, 3, g:g + 1]}
                for ev in events or od.events:
                    if ev[0] == "last_turn":
                        act.wait_ge(turned, 2 * NC)
                        high_part(3 * NC - 1, VALUES)
                    if ev[0] == "scores":
                        _, n, k, h = ev
                        t = od.tile_at[n, k, h]
                        w = od.key_tiles(n)[k][1]
                        act.wait_ge(S[kind, "scores_ready"], t + 1)
                        if t >= SLOTS:
                            key = (t - SLOTS) // G
                            if od.a:
                                act.wait_ge(ones_done, key // 2 + 1)
                            else:
                                act.wait_ge(S[kind, "values_done"], key + 1)
                        nc.scalar.activation(prob[:, t % SLOTS, 0:w], ps[:, t % BANKS, 0:w], ACT.Exp,
                                             scale=float((DA if od.a else DB) ** -0.5)).then_inc(S[kind, "exp_done"], 1)
                    elif ev[0] == "evacuate":
                        n = ev[1]
                        act.wait_ge(S[kind, "values_done"], od.key_at[n, len(od.key_tiles(n)) - 1] + 1)
                        if n:
                            act.wait_ge(S[kind, "weighed"], n)
                        nc.scalar.activation(o_sb[:], ps[:, VALUES, :], ACT.Identity).then_inc(S[kind, "evacuated"], 1)
                    elif ev[0] == "ring" and ev[1][0] == "turn":
                        act.wait_ge(S[kind, "ring_full"], od.at[ev[1]] + 1)
                        high_part(NC * r + ev[1][1], bank_of(kind, od.at[ev[1]]))
                    elif ev[0] == "ring" and od.freer(ev[1]) == "activation":
                        use = ev[1]
                        m = od.at[use]
                        act.wait_ge(S[kind, "ring_full"], m + 1)
                        if use[0] == "v":
                            _, g, c = use
                            dst = vst[:, g % 2, c * TPC:(c + 1) * TPC, :]
                            src = ps[:, bank_of(kind, m), :].rearrange("p (t d) -> p t d", d=P)
                        else:
                            dst, src = q_slot(od, *use[1:])[CA:CA + 2, :], ps[CA:CA + 2, bank_of(kind, m), :]
                        nc.scalar.activation(dst, src, ACT.Identity).then_inc(S[kind, "freed_by_activation"], 1)
                    elif ev[0] == "ring" and ev[1] in od.proj_at:
                        use = ev[1]
                        m, j = od.at[use], od.proj_at[use]
                        rows = P if (use[0] == "lat" or not od.a) else KA_ROWS
                        act.wait_ge(S[kind, "ring_full"], m + 1)
                        if j >= 2:
                            before = [u for u, i in od.proj_at.items() if i == j - 2][0]
                            wait_freed(act, kind, *before)
                        if od.a:
                            mark = col({"q": "lo_qa", "k": "lo_ka", "lat": "lo_lat"}[use[0]], rows)
                            add = 0.0
                        else:
                            g = od.steps[use[1]][0] if use[0] == "q" else use[1]
                            mark = col("lo_qb" if use[0] == "q" else "lo_kb")
                            add = bias_cols[use[0]](g)
                        nc.scalar.activation(tmp[0:rows, j % 2, :], ps[0:rows, bank_of(kind, m), :], ACT.Identity,
                                             scale=mark, bias=add).then_inc(S[kind, "high_ready"], 1)

            def ffn(r):
                def exp_of_logits(c):
                    act.wait_ge(logits_shifted, NC * r + c + 1)
                    t = slice(c * TPC, (c + 1) * TPC)
                    nc.scalar.activation(pr[:, t, :], lg[:, t, :], ACT.Exp).then_inc(exp_logits, 1)

                def turn(c):
                    act.wait_ge(turned, NC * (r + 1) + c + 1)
                    high_part(NC * (2 * r + 2) + c, 7 - c % 2)

                def unit(e, c, more):
                    i = NC * e + c
                    for f, (_, rows) in enumerate(FT):
                        j = (UNITS * r + i) * len(FT) + f
                        act.wait_ge(gate_ready, plus(j + 1, more, JOBS))
                        if j >= 2:
                            act.wait_ge(hidden_ready, plus(j - 1, more, JOBS))
                        nc.scalar.activation(silu[0:rows, j % 2, :], ps[0:rows, j % 2, :], ACT.Silu).then_inc(silu_done, 1)
                        if tail_after(i, f) is not None:
                            attention("AB"[r], 2 * r + 1, orders["AB"[r]].tail[tail_after(i, f)])
                    if i == NC:
                        for chunk in range(NC):
                            exp_of_logits(chunk)
                    if r == 0 and e == NEXP - 1 and c >= 2:
                        turn(c - 2)

                walk_units(act, unit)
                if r == 0:
                    turn(2)

            act.wait_ge(loaded["cst"], 16)
            for c in range(NC):
                act.wait_ge(turned, c + 1)
                high_part(c, START_BANKS[c])
            attention("A", 1)
            ffn(0)
            act.wait_ge(biases_ready, 1)
            attention("B", 3)
            ffn(1)

        @block.vector
        def _(v):
            n_chain = [0]

            def link(ins):
                ins.then_inc(chain, 1)
                n_chain[0] += 1
                v.wait_ge(chain, n_chain[0])

            def norm_a(i):
                c = i % NC
                for t in range(c * TPC, (c + 1) * TPC):
                    last = nc.vector.bn_stats(stats[:, t, :], x[:, t, :])
                link(last)
                for t in range(c * TPC, (c + 1) * TPC):
                    last = nc.vector.bn_aggr(mv[:, t, :], stats[:, t, :])
                link(last)
                t = slice(c * TPC, (c + 1) * TPC)
                nc.vector.tensor_scalar(ve[:, t], mv[:, t, 1], EPS, None, ALU.add).then_inc(var_ready, 1)

            def norm_b(i):
                c = i % NC
                t = slice(c * TPC, (c + 1) * TPC)
                v.wait_ge(root_ready, i + 1)
                link(nc.vector.tensor_tensor(newton[:], rs[:, t], rs[:, t], ALU.mult))
                link(nc.vector.tensor_tensor(newton[:], newton[:], ve[:, t], ALU.mult))
                link(nc.vector.tensor_scalar(newton[:], newton[:], -0.5, 1.5, ALU.mult, ALU.add))
                link(nc.vector.tensor_tensor(rs[:, t], rs[:, t], newton[:], ALU.mult))
                for q in range(TPC):
                    t = c * TPC + q
                    last = nc.vector.tensor_scalar(xn[:, c % 2, q, :], x[:, t, :], mv[:, t, 0:1], rs[:, t:t + 1],
                                                   ALU.subtract, ALU.mult)
                last.then_inc(norm_ready, 1)

            def low_part(i, bank, signal):
                c = i % NC
                v.wait_ge(high_done, i + 1)
                nc.vector.tensor_tensor(xl[:, c * QC:(c + 1) * QC], ps[:, bank, :],
                                        xh[:, c * QC:(c + 1) * QC].bitcast(F32), ALU.subtract).then_inc(signal, 1)

            def attention(kind, r, events=None):
                od = orders[kind]
                full, free = S[kind, "ring_full"], S[kind, "freed_by_vector"]
                for ev in events or od.events:
                    if ev[0] == "last_turn":
                        low_part(3 * NC - 1, VALUES, parts_done)
                    if ev[0] == "first_expert":
                        split_expert(v, nc.vector, r // 2, 0)
                    if ev[0] == "scores" and od.adder(*ev[1:]) == "vector":
                        add_pair(v, nc.vector, od, *ev[1:])
                    if ev[0] == "norm_a":
                        n = [m for m, s in enumerate(od.steps) if s == (od.groups - 1, ev[1])][0]
                        wait_freed(v, kind, "out", n)
                        norm_a(NC * r + ev[1])
                    if ev[0] == "norm_b":
                        if ev[1] >= 2:
                            v.wait_ge(full, od.at["turn", ev[1] - 2] + 1)
                        norm_b(NC * r + ev[1])
                    if ev[0] == "weigh":
                        n = ev[1]
                        if n:
                            v.wait_ge(S[kind, "weighed"], n)
                        if od.a:
                            v.wait_ge(ones_done, (n + 1) * NT // 2)
                            sums, row = ps[:, ONES, :], 0
                        else:
                            v.wait_ge(S[kind, "evacuated"], n + 1)
                            sums, row = o_sb[:], DB
                        link(nc.vector.transpose(rinv[:], sums))
                        link(nc.vector.reciprocal(rc[:], rinv[:].rearrange("p (b r) -> p b r", r=32)[:, :, row]))
                        nc.vector.transpose(rinv[:], rc[:].rearrange("p (b r) -> p b r", r=1).broadcast_to([P, QC // 32, 32]))\
                            .then_inc(S[kind, "inverted"], 1)
                    if ev[0] == "scale" and ev[1] == len(od.steps) - 1:
                        v.wait_ge(S[kind, "evacuated"], ev[1] + 1)
                        v.wait_ge(S[kind, "inverted"], ev[1] + 1)
                        nc.vector.tensor_tensor(ot[:], o_sb[:], rinv[:], ALU.mult).then_inc(S[kind, "weighed"], 1)
                    if ev[0] != "ring" or od.freer(ev[1]) != "vector":
                        continue
                    use = ev[1]
                    m = od.at[use]
                    bank = bank_of(kind, m)
                    v.wait_ge(full, m + 1)
                    if use in od.proj_at:
                        j = od.proj_at[use]
                        v.wait_ge(S[kind, "high_ready"], j + 1)
                        if use[0] == "lat":
                            c = use[1]
                            dst, rows, add = flat[:, c * QC:(c + 1) * QC], P, col("zero")
                        elif use[0] == "k" and od.a:
                            _, g, h, c = use
                            rows, add = KA_ROWS, col("neg_ka", KA_ROWS)
                            dst = kst[0:rows, g % 2, h, c * QC:(c + 1) * QC]
                        elif use[0] == "k":
                            _, g, _, c = use
                            if g and c == 0:
                                v.wait_ge(S[kind, "keys_ready"], 16 * G * g)
                            dst, rows, add = flat[:, c * QC:(c + 1) * QC], P, bias[:, 1, g:g + 1]
                        else:
                            _, n, h = use
                            rows = KA_ROWS if od.a else P
                            add = col("zero", rows) if od.a else bias[:, 0, od.steps[n][0]:od.steps[n][0] + 1]
                            dst = q_slot(od, n, h)[0:rows, :]
                            if n >= Q_STEPS[kind]:
                                v.wait_ge(S[kind, "scores_ready"], od.tile_at[n - Q_STEPS[kind] + 1, 0, 0])
                        nc.vector.scalar_tensor_tensor(dst, ps[0:rows, bank, :], add, tmp[0:rows, j % 2, :].bitcast(F32),
                                                       ALU.add, ALU.subtract).then_inc(free, 1)
                    elif use[0] == "v":
                        _, g, c = use
                        dst = vst[:, g % 2, c * TPC:(c + 1) * TPC, :]
                        if g >= 2 and c == 0:
                            v.wait_ge(S[kind, "values_done"], od.last_key_of_group[g - 2])
                        width = G * DB
                        for q in range(TPC):
                            ins = nc.vector.tensor_tensor(
                                dst[:, q, :].rearrange("p (h r) -> p h r", r=32)[:, :, 0:DB],
                                ps[:, bank, q * width:(q + 1) * width].rearrange("p (h r) -> p h r", r=DB),
                                bv_sb[:, g * width:(g + 1) * width].rearrange("p (h r) -> p h r", r=DB), ALU.add)
                        ins.then_inc(free, 1)
                    elif use[0] == "max":
                        _, n, h, q, k = use
                        first = od.first_key_chunk(n)
                        lo = P * q if (not od.a and k == first) else 0
                        nc.vector.reduce_max(mx[:, h, q, k:k + 1], ps[:, bank, lo:QC], AX.X).then_inc(free, 1)
                        if q == TPC - 1 and k == NC - 1 and (od.a or h == G - 1):
                            v.wait_ge(free, od.freed_at[use] + 1)
                            hs = slice(h, h + 1) if od.a else slice(0, G)
                            link(nc.vector.reduce_max(mq[:, n % 2, hs, :], mx[:, hs, :, first:NC], AX.X))
                            before = ("shift", n - 2, 0) if not od.a else ("shift", n, h - 2) if h >= 2 else ("shift", n - 1, h + 2)
                            if before[1] >= 0:
                                v.wait_ge(full, od.at[before] + 1)
                            if od.a:
                                columns = ct[:, h % 2:h % 2 + 1, :, CA:CA + 2]
                            else:
                                columns = ct[:, n % 2, :, :].rearrange("p t (h r) -> p h t r", r=32)[:, :, :, CB:CB + 2]
                            hi, lo_part = columns[:, :, :, 0], columns[:, :, :, 1]
                            link(nc.vector.tensor_copy(hi, mq[:, n % 2, hs, :]))
                            nc.vector.tensor_tensor(lo_part, mq[:, n % 2, hs, :], hi.bitcast(F32), ALU.subtract)\
                                .then_inc(S[kind, "shift_parts"], 1)
                    elif use[0] == "shift":
                        dst = q_slot(od, *use[1:])
                        nc.vector.tensor_tensor(dst, ps[:, bank, :], dst.bitcast(F32), ALU.add).then_inc(free, 1)
                    elif use[0] == "turn":
                        low_part(NC * r + use[1], bank, free)
                    elif use[0] == "out":
                        c = od.steps[use[1]][1]
                        if not od.a and use[1] == 0:
                            v.wait_ge(bias_added, 1)
                        xs = x[:, c * TPC:(c + 1) * TPC, :]
                        nc.vector.tensor_tensor(xs, ps[:, bank, :].rearrange("p (t d) -> p t d", d=P), xs, ALU.add)\
                            .then_inc(free, 1)
                    if ev == ("ring", ("out", len(od.steps) - 1)):
                        wait_freed(v, kind, *use)
                        nc.vector.memset(marker[:, 0:1], 0.0).then_inc(attention_done, 1)
                        v.wait_ge(attention_done, 1 if od.a else 2)

            def b_biases():
                v.wait_ge(loaded["b"], 128)
                v.wait_ge(filled, 4)
                link(nc.vector.tensor_scalar(bias[:, 2, :], bias[:, 0, :], col("lo_qb"), None, ALU.mult))
                nc.vector.tensor_scalar(bias[:, 3, :], bias[:, 1, :], col("lo_kb"), None, ALU.mult).then_inc(biases_ready, 1)
                v.wait_ge(biases_ready, 1)
                link(nc.vector.tensor_scalar(bias[:, 1, :], bias[:, 1, :], col("neg_kb"), None, ALU.add))

            def ffn(r):
                wide = [P, TPC, E]

                def route_a(c):
                    t = slice(c * TPC, (c + 1) * TPC)
                    v.wait_ge(logits_ready, NC * r + c + 1)
                    nc.vector.tensor_copy(lg[:, t, :], ps[:, 6 + c % 2, 0:TPC * E].rearrange("p (t e) -> p t e", e=E))\
                        .then_inc(logits_taken, 1)
                    v.wait_ge(logits_taken, NC * r + c + 1)
                    link(nc.vector.reduce_max(lmax[:, t], lg[:, t, :], AX.X))
                    nc.vector.tensor_tensor(lg[:, t, :], lg[:, t, :], lmax[:, t].rearrange("p (t a) -> p t a", a=1)
                                            .broadcast_to(wide), ALU.subtract).then_inc(logits_shifted, 1)

                def route_b(c):
                    t = slice(c * TPC, (c + 1) * TPC)
                    lsum, lrec = lmax[:, t], lrecip[:, t]

                    def spread(a, n=E):
                        return a.broadcast_to([P, TPC, n])

                    v.wait_ge(exp_logits, NC * r + c + 1)
                    link(nc.vector.reduce_sum(lsum, pr[:, t, :], AX.X))
                    link(nc.vector.reciprocal(lrec, lsum))
                    link(nc.vector.tensor_tensor(pr[:, t, :], pr[:, t, :], spread(lrec.rearrange("p (t a) -> p t a", a=1)),
                                                 ALU.mult))
                    for q in range(c * TPC, (c + 1) * TPC):
                        last = nc.vector.max(top[:, q, :], pr[:, q, :])
                    link(last)
                    for q in range(c * TPC, (c + 1) * TPC):
                        last = nc.vector.max_index(topi[:, q, :], top[:, q, :], pr[:, q, :])
                    link(last)
                    nc.vector.tensor_copy(topf[:, t, :], topi[:, t, 0:2])
                    link(nc.vector.tensor_tensor(lsum, top[:, t, 0], top[:, t, 1], ALU.add))
                    link(nc.vector.reciprocal(lrec, lsum))
                    link(nc.vector.tensor_tensor(wtop[:, t, :], top[:, t, 0:2],
                                                 spread(lrec.rearrange("p (t a) -> p t a", a=1), 2), ALU.mult))
                    iota = cst[:, C_IOTA:C_IOTA + E].rearrange("p (a e) -> p a e", a=1).broadcast_to(wide)
                    for i, dst in enumerate((cw[:, t, :], cw2[:, t, :])):
                        link(nc.vector.tensor_tensor(dst, iota, spread(topf[:, t, i:i + 1]), ALU.is_equal))
                        link(nc.vector.tensor_tensor(dst, dst, spread(wtop[:, t, i:i + 1]), ALU.mult))
                    link(nc.vector.tensor_tensor(cw[:, t, :], cw[:, t, :], cw2[:, t, :], ALU.add))

                def add_down(i, more):
                    e, c = divmod(i, NC)
                    y = UNITS * r + i
                    v.wait_ge(down_ready, plus(y + 1, more, NC))
                    if e:
                        v.wait_ge(added, plus(y - NC + 1, more, NC))
                    for q in range(TPC):
                        t = c * TPC + q
                        src = ps[:, 4 + y % 2, q * P:(q + 1) * P]
                        if e == 0:
                            ins = nc.vector.tensor_tensor(x[:, t, :], src, x[:, t, :], ALU.add)
                        else:
                            ins = nc.vector.scalar_tensor_tensor(x[:, t, :], src, cw[:, t, bass.ds(plus(e - 1, more, 1), 1)], x[:, t, :],
                                                                 ALU.mult, ALU.add)
                    ins.then_inc(added, 1)

                def norm_a_after(c):
                    v.wait_ge(added, UNITS * r + (NEXP - 1) * NC + c + 1)
                    norm_a(2 * NC + c)

                def norm_b_after(c):
                    if c >= 2:
                        v.wait_ge(turned, NC + c - 1)
                    norm_b(2 * NC + c)

                def unit(e, c, more):
                    i = NC * e + c
                    y = UNITS * r + i
                    for f, (_, rows) in enumerate(FT):
                        j = y * len(FT) + f
                        v.wait_ge(silu_done, plus(j + 1, more, JOBS))
                        v.wait_ge(up_ready, plus(j + 1, more, JOBS))
                        if f == 0 and y >= 2:
                            v.wait_ge(down_ready, plus(y - 1, more, NC))
                        nc.vector.tensor_tensor(hid[0:rows, y % 2, f, :], ps[0:rows, 2 + j % 2, :],
                                                silu[0:rows, j % 2, :], ALU.mult).then_inc(hidden_ready, 1)
                        if tail_after(i, f) is not None:
                            attention("AB"[r], 2 * r + 1, orders["AB"[r]].tail[tail_after(i, f)])
                        if f == 1 and i:
                            add_down(i - 1, more)
                            if r == 0 and e == NEXP - 1 and c:
                                norm_a_after(c - 1)
                    if r == 0 and i == UNITS - NC:
                        b_biases()
                    if e == 0:
                        route_a(c)
                    if e == 1:
                        route_b(c)
                    if r == 0 and e == NEXP - 1:
                        if c >= 1:
                            norm_b_after(c - 1)
                        if c >= 2:
                            low_part(2 * NC + c - 2, 7 - c % 2, parts_done)

                walk_units(v, unit)
                add_down(UNITS - 1, 0)
                if r == 0:
                    norm_a_after(NC - 1)
                    low_part(2 * NC + 2, 7, parts_done)
                    norm_b_after(NC - 1)
                v.wait_ge(added, UNITS * (r + 1))

            v.wait_ge(loaded["cst"], 16)
            for c in range(NC + 2):
                for ahead in (0, 1) if c == 0 else (c + 1,):
                    if ahead < NC:
                        v.wait_ge(loaded["x"][ahead], 16)
                        norm_a(ahead)
                if c < NC:
                    if c >= 2:
                        v.wait_ge(turned, c - 1)
                    norm_b(c)
                if c >= 2:
                    low_part(c - 2, START_BANKS[c - 2], parts_done)
            v.wait_ge(loaded["masks"], 16)
            nc.vector.tensor_copy(identr[:], ident)
            link(nc.vector.tensor_copy(maskr[:], mask_raw))
            v.wait_ge(filled, 3)
            attention("A", 1)
            ffn(0)
            attention("B", 3)
            ffn(1)

        @block.tensor
        def _(pe):
            mm = nc.tensor.matmul

            def turn(i, bank):
                pe.wait_ge(norm_ready, i + 1)
                c = i % NC
                for q in range(TPC):
                    last = nc.tensor.transpose(ps[:, bank, q * P:(q + 1) * P], xn[:, c % 2, q, :], ident)
                return last

            def three(dst, wh, wl, xs, start=True, stop=True):
                a, b = xs
                mm(dst, wh, a, start=start, stop=False)
                mm(dst, wh, b, start=False, stop=False)
                return mm(dst, wl, a, start=False, stop=stop)

            def attention(kind, r, events=None):
                od = orders[kind]
                full = S[kind, "ring_full"]
                depth = len(RING[kind])
                first_uses = {("lat", 0): "wc", ("k", 0, 0, 0): "wk", ("v", 0, 0): "wv", ("q", 0, 0): "wq"}
                for ev in events or od.events:
                    if ev[0] == "last_turn":
                        turn(3 * NC - 1, VALUES).then_inc(turned, 1)
                    if not od.a and ev[0] == "ring" and ev[1][0] in ("k", "v") and ev[1][1] == 0:
                        wait_parts(pe, 2, ev[1][-1])
                        if od.at[ev[1]] == RING["B"].index(START_TURN_BANK):
                            wait_parts(pe, 2, NC - 2)
                    if ev[0] == "scores":
                        _, n, k, h = ev
                        g, c = od.steps[n]
                        t = od.tile_at[n, k, h]
                        if t >= BANKS:
                            pe.wait_ge(S[kind, "exp_done"], t - BANKS + 1)
                        if k == 0:
                            wait_freed(pe, kind, "shift", n, h if od.a else 0)
                        rows = KA_ROWS if od.a else P
                        rhs = q_slot(od, n, h)[0:rows, :]
                        kt, w, diagonal = od.key_tiles(n)[k]
                        dst = ps[:, t % BANKS, 0:w]
                        last = mm(dst, kst[0:rows, g % 2, h, kt * P:(kt + 1) * P], rhs[:, 0:w],
                                  start=True, stop=not diagonal)
                        if diagonal:
                            last = mm(dst[:, w - P:w], identr[:], maskr[:, 0, :], start=False, stop=True)
                        last.then_inc(S[kind, "scores_ready"], 1)
                    elif ev[0] == "values":
                        _, n, k = ev
                        g, c = od.steps[n]
                        keys = od.key_tiles(n)
                        key = od.key_at[n, k]
                        kt, w, _ = keys[k]
                        pe.wait_ge(S[kind, "exp_done"], G * (key + 1))
                        if k == 0:
                            if n:
                                pe.wait_ge(S[kind, "evacuated"], n)
                            wait_freed(pe, kind, "v", g, NC - 1)
                        for h in range(G):
                            last = mm(ps[32 * h:32 * h + 32, VALUES, 0:w], vst[:, g % 2, kt, 32 * h:32 * h + 32],
                                      prob[:, (G * key + h) % SLOTS, 0:w], start=k == 0, stop=k == len(keys) - 1)
                        last.then_inc(S[kind, "values_done"], 1)
                    elif ev[0] == "ones":
                        pair = ev[1]
                        n, k = divmod(pair, NT // 2)
                        by_vector = G // 2 * (k + 1) if n == len(od.steps) - 1 else 0
                        pe.wait_ge(pair_summed["pool"], G * (pair + 1) - by_vector)
                        if by_vector:
                            pe.wait_ge(pair_summed["vector"], by_vector)
                        if k == 0 and n:
                            pe.wait_ge(S[kind, "inverted"], n)
                        for h in range(G):
                            last = mm(ps[32 * h:32 * h + 32, ONES, :], ones[:], prob[:, (2 * G * pair + h) % SLOTS, :],
                                      start=k == 0, stop=k == NT // 2 - 1)
                        last.then_inc(ones_done, 1)
                    elif ev[0] == "ring":
                        use = ev[1]
                        m = od.at[use]
                        bank = bank_of(kind, m)
                        if od.a and use in first_uses:
                            pe.wait_ge(weights_split, split_count(first_uses[use]))
                        if m >= depth and not events:
                            wait_freed(pe, kind, *od.use_at[m - depth])
                        if use[0] == "turn":
                            last = turn(NC * r + use[1], bank)
                        elif use[0] == "lat":
                            c = use[1]
                            wait_parts(pe, 0, c)
                            xs = (xh[:, c * QC:(c + 1) * QC], xl[:, c * QC:(c + 1) * QC])
                            last = three(ps[:, bank, :], wch[:], wcl[:], xs)
                        elif use[0] == "k" and od.a:
                            _, g, h, c = use
                            wait_freed(pe, kind, "lat", NC - 1)
                            dst, rhs = ps[0:KA_ROWS, bank, :], flat[:, c * QC:(c + 1) * QC]
                            mm(dst, wkh[:, g * G + h, :], rhs, start=True, stop=False)
                            last = mm(dst, wkl[:, g * G + h, :], rhs, start=False, stop=True)
                        elif use[0] == "v":
                            _, g, c = use
                            for q in range(TPC) if od.a else []:
                                lhs = flat[:, c * QC + q * P:c * QC + (q + 1) * P]
                                dst = ps[:, bank, q * P:(q + 1) * P]
                                mm(dst, lhs, wvh[:, g * P:(g + 1) * P], start=True, stop=False)
                                last = mm(dst, lhs, wvl[:, g * P:(g + 1) * P], start=False, stop=True)
                            for q in [] if od.a else range(TPC):
                                s = slice(c * QC + q * P, c * QC + (q + 1) * P)
                                w = slice(g * G * DB, (g + 1) * G * DB)
                                dst = ps[:, bank, q * G * DB:(q + 1) * G * DB]
                                mm(dst, xh[:, s], wvbh[:, w], start=True, stop=False)
                                mm(dst, xl[:, s], wvbh[:, w], start=False, stop=False)
                                last = mm(dst, xh[:, s], wvbl[:, w], start=False, stop=True)
                        elif use[0] == "k":
                            _, g, _, c = use
                            xs = (xh[:, c * QC:(c + 1) * QC], xl[:, c * QC:(c + 1) * QC])
                            last = three(ps[:, bank, :], wkbh[:, g, :], wkbl[:, g, :], xs)
                        elif use[0] == "q":
                            _, n, h = use
                            g, c = od.steps[n]
                            xs = (xh[:, c * QC:(c + 1) * QC], xl[:, c * QC:(c + 1) * QC])
                            if od.a:
                                last = three(ps[0:KA_ROWS, bank, :], wqh[:, g * G + h, :], wql[:, g * G + h, :], xs)
                            else:
                                last = three(ps[:, bank, :], wqbh[:, g, :], wqbl[:, g, :], xs)
                        elif use[0] == "max":
                            _, n, h, q, k = use
                            g, c = od.steps[n]
                            if q == 0 and k == od.first_key_chunk(n):
                                wait_freed(pe, kind, "q", n, h if od.a else 0)
                                if od.a:
                                    wait_freed(pe, kind, "k", g, G - 1, NC - 1)
                                else:
                                    pe.wait_ge(S[kind, "keys_ready"], 16 * G * (g + 1))
                            rows = CA if od.a else P
                            diagonal = not od.a and k == c
                            lo = P * q if diagonal else 0
                            lhs = q_slot(od, n, h)[0:rows, q * P:(q + 1) * P]
                            last = mm(ps[:, bank, lo:QC], lhs, kst[0:rows, g % 2, h, k * QC + lo:(k + 1) * QC],
                                      start=True, stop=not diagonal)
                            if diagonal:
                                last = mm(ps[:, bank, lo:lo + P], identr[:], maskr[:, 1, :], start=False, stop=True)
                        elif use[0] == "shift":
                            _, n, h = use
                            if od.a:
                                pe.wait_ge(S[kind, "shift_parts"], G * n + h + 1)
                                rows, par = KA_ROWS, h % 2
                            else:
                                pe.wait_ge(S[kind, "shift_parts"], n + 1)
                                rows, par = P, n % 2
                            for q in range(TPC):
                                last = mm(ps[0:rows, bank, q * P:(q + 1) * P], ct[:, par, q, 0:rows], identr[:],
                                          start=True, stop=True)
                        elif use[0] == "out":
                            n = use[1]
                            g, c = od.steps[n]
                            pe.wait_ge(S[kind, "weighed"], n + 1)
                            for q in range(TPC):
                                last = mm(ps[:, bank, q * P:(q + 1) * P], ot[:, q * P:(q + 1) * P],
                                          wo_sb[:, g, :], start=True, stop=True)
                        last.then_inc(full, 1)

            def ffn(r):
                def logits(c):
                    if c == 0 and r == 0:
                        pe.wait_ge(weights_split, split_count("gw"))
                    if c >= 2 or r:
                        pe.wait_ge(logits_taken, NC * r + c - 1)
                    if c == TAIL_OUT - 6:
                        wait_freed(pe, "AB"[r], "out", len(orders["AB"[r]].steps) - 1)
                    for q in range(TPC):
                        s = slice(c * QC + q * P, c * QC + (q + 1) * P)
                        dst = ps[:, 6 + c % 2, q * E:(q + 1) * E]
                        mm(dst, xh[:, s], gwh[:], start=True, stop=False)
                        mm(dst, xl[:, s], gwh[:], start=False, stop=False)
                        mm(dst, xh[:, s], gwl[:], start=False, stop=False)
                        last = mm(dst, xl[:, s], gwl[:], start=False, stop=True)
                    last.then_inc(logits_ready, 1)

                def down(i, more):
                    y = UNITS * r + i
                    pe.wait_ge(hidden_ready, plus((y + 1) * len(FT), more, JOBS))
                    if y >= 2:
                        pe.wait_ge(added, plus(y - 1, more, NC))
                    if i == TAIL_TURN - 4:
                        wait_freed(pe, "AB"[r], "turn", NC - 1)
                    for q in range(TPC):
                        for f, (_, rows) in enumerate(FT):
                            last = mm(ps[:, 4 + y % 2, q * P:(q + 1) * P], hid[0:rows, y % 2, f, q * P:(q + 1) * P],
                                      wd[i // NC % 2][0:rows, f, :], start=f == 0, stop=f == len(FT) - 1)
                    last.then_inc(down_ready, 1)

                def turn_after(c):
                    if c >= 2:
                        pe.wait_ge(parts_done, NC + c - 1)
                    turn(2 * NC + c, 7 - c % 2).then_inc(turned, 1)

                kind = "AB"[r]
                pe.wait_ge(S[kind, "exp_done"], orders[kind].tiles)
                wait_all_freed(pe, kind)

                def unit(e, c, more):
                    i = NC * e + c
                    n = NEXP * r + e
                    if c == 0:
                        pe.wait_ge(gu_split, plus(2 * (n + 1), more, 2))
                        pe.wait_ge(gu_loaded[e % 2], plus(48 * loads_of(r, e), more, 24))
                    if i == NC - 1:
                        wait_freed(pe, kind, "turn", c)
                    xs = (xh[:, c * QC:(c + 1) * QC], xl[:, c * QC:(c + 1) * QC])
                    for f, (at, rows) in enumerate(FT):
                        j = (UNITS * r + i) * len(FT) + f
                        if j >= 2:
                            pe.wait_ge(silu_done, plus(j - 1, more, JOBS))
                        three(ps[0:rows, j % 2, :], wguh[e % 2][:, at:at + rows], wgul[e % 2][:, at:at + rows], xs)\
                            .then_inc(gate_ready, 1)
                        if j >= 2:
                            pe.wait_ge(hidden_ready, plus(j - 1, more, JOBS))
                        three(ps[0:rows, 2 + j % 2, :], wguh[e % 2][:, I + at:I + at + rows],
                              wgul[e % 2][:, I + at:I + at + rows], xs).then_inc(up_ready, 1)
                        if f == 0 and i:
                            down(i - 1, more)
                        if tail_after(i, f) is not None:
                            attention(kind, 2 * r + 1, orders[kind].tail[tail_after(i, f)])
                    if e == 0:
                        logits(c)
                    if r == 0 and e == NEXP - 1 and c >= 2:
                        turn_after(c - 2)

                walk_units(pe, unit)
                down(UNITS - 1, 0)
                if r == 0:
                    turn_after(2)

            pe.wait_ge(loaded["cst"], 16)
            for c in range(NC):
                turn(c, START_BANKS[c]).then_inc(turned, 1)
            pe.wait_ge(filled, 3)
            attention("A", 1)
            ffn(0)
            pe.wait_ge(weights_split, split_count("wvb"))
            pe.wait_ge(filled, 7)
            pe.wait_ge(added, UNITS)
            attention("B", 3)
            ffn(1)


def stack_heads(w, heads, width, parts, pitch):
    w = w.reshape(w.shape[0], heads, width)
    zero = np.zeros((w.shape[0], heads, pitch - parts * width), w.dtype)
    return np.concatenate([w] * parts + [zero], axis=2)


def kernel(L0_attn_a_x, L0_attn_a_Wq, L0_attn_a_Wkv_down, L0_attn_a_Wk_up, L0_attn_a_Wv_up, L0_attn_a_Wo,
           L0_attn_b_w_qkv, L0_attn_b_b_qkv, L0_attn_b_w_out, L0_attn_b_b_out, L0_ffn_gate_w,
           L0_ffn_base_wgu, L0_ffn_base_wd, L0_ffn_exp_wgu, L0_ffn_exp_wd):
    import concourse.bacc as bacc
    from concourse.bass_utils import run_bass_kernel_spmd

    f = lambda a: np.asarray(a)
    x = f(L0_attn_a_x).reshape(T, D)
    wqkv, bqkv = f(L0_attn_b_w_qkv), f(L0_attn_b_b_qkv)
    b3 = bqkv.reshape(3, 1, D)
    bias_cols = lambda b: stack_heads(b, HB, DB, 3, 32).reshape(GB, P).T
    wob = f(L0_attn_b_w_out).reshape(HB, DB, D)
    wob = np.concatenate([wob, np.zeros((HB, 32 - DB, D), wob.dtype)], axis=1)
    wk = f(L0_attn_a_Wk_up).T
    wv = f(L0_attn_a_Wv_up).T
    kv = f(L0_attn_a_Wkv_down).T
    arrays = {
        "x": x,
        "wq_a": stack_heads(f(L0_attn_a_Wq).T, HA, DA, 3, KA_ROWS),
        "wkv_a": np.concatenate([kv, kv], axis=1),
        "wk_a": stack_heads(np.concatenate([wk, wk], axis=0), HA, DA, 3, KA_ROWS),
        "wv_a": np.concatenate([wv, wv], axis=0),
        "wo_a": f(L0_attn_a_Wo).T.reshape(GA, P, D).transpose(1, 0, 2),
        "wq_b": stack_heads(wqkv[:, 0:D], HB, DB, 3, 32).reshape(D, GB, P),
        "wk_b": stack_heads(wqkv[:, D:2 * D], HB, DB, 3, 32).reshape(D, GB, P),
        "wv_b": wqkv[:, 2 * D:3 * D],
        "bq_b": bias_cols(b3[0]),
        "bk_b": bias_cols(b3[1]),
        "bv_b": b3[2],
        "wo_b": wob.reshape(GB, P, D).transpose(1, 0, 2),
        "bo_b": f(L0_attn_b_b_out).reshape(1, D),
        "gate_w": f(L0_ffn_gate_w),
        "base_wgu": f(L0_ffn_base_wgu),
        "base_wd": f(L0_ffn_base_wd),
        "exp_wgu": f(L0_ffn_exp_wgu),
        "exp_wd": f(L0_ffn_exp_wd),
        "consts": constants(),
        "masks": diagonal_masks(),
    }
    arrays = {n: np.ascontiguousarray(a) for n, a in arrays.items()}
    nc = bacc.Bacc("TRN2", target_bir_lowering=False, num_devices=1)
    args = [nc.dram_tensor("in_" + n, a.shape, mybir.dt.from_np(a.dtype), kind="ExternalInput").ap()
            for n, a in arrays.items()]
    out = nc.dram_tensor("out_x", (T, D), F32, kind="ExternalOutput").ap()
    build(nc, *args, out)
    r = run_bass_kernel_spmd(nc, [{"in_" + n: a for n, a in arrays.items()}], core_ids=[0])
    return r.results[0]["out_x"].reshape(1, T, D)
```
